# Optimizing a Trainium2 kernel written in Bass

```python
import numpy as np
import jax
import jax.numpy as jnp

def _softmax(x, axis=-1):
    return jax.nn.softmax(x, axis=axis)

def _gelu(x):
    return jax.nn.gelu(x, approximate=True)

def _silu(x):
    return jax.nn.silu(x)

def _sigmoid(x):
    return jax.nn.sigmoid(x)

def _layernorm(x, axis=-1, eps=1e-05):
    m = jnp.mean(x, axis=axis, keepdims=True)
    v = jnp.var(x, axis=axis, keepdims=True)
    return (x - m) / jnp.sqrt(v + eps)

def _scatter_add(tgt, idx, src, axis=0):
    return tgt.at[idx].add(src)

def _segment_sum(src, seg, n):
    return jax.ops.segment_sum(src, seg, n)
kernel_name = 'mk_conv_seq_d2_conv_nhwc512_r2_66afb5'

def setup_inputs(seed: int=0):
    np.random.seed(seed)
    _w = jnp.asarray

    def _rec_inputs():
        import jax
        import jax.numpy as jnp
        _gk = jax.random.key(seed)
        x = -0.0002928 + 1 * jax.random.normal(jax.random.fold_in(_gk, 1), (2, 32, 32, 256), jnp.float32)
        return x
    x = _rec_inputs()

    def _L0_conv_setup():
        import jax, jax.numpy as jnp
        import numpy as np
        GROUPS = 32
        EPS = 1e-05

        def group_norm(x, gamma, beta):
            B, H, W, C = x.shape
            xg = x.reshape(B, H, W, GROUPS, C // GROUPS)
            mean = xg.mean(axis=(1, 2, 4), keepdims=True)
            var = xg.var(axis=(1, 2, 4), keepdims=True)
            xn = ((xg - mean) * jax.lax.rsqrt(var + EPS)).reshape(B, H, W, C)
            return xn * gamma + beta

        def conv1x1(x, w, b):
            return jnp.einsum('bhwc,cd->bhwd', x, w) + b
        key = jax.random.key(seed)
        ks = jax.random.split(key, 10)
        C = 256
        s = 1.0 / np.sqrt(C)
        inp = {'x': jax.random.normal(ks[0], (2, 32, 32, C), dtype=jnp.float32), 'gamma': jnp.ones((C,), jnp.float32), 'beta': jnp.zeros((C,), jnp.float32), 'wq': jax.random.normal(ks[1], (C, C), jnp.float32) * s, 'bq': jnp.zeros((C,), jnp.float32), 'wk': jax.random.normal(ks[2], (C, C), jnp.float32) * s, 'bk': jnp.zeros((C,), jnp.float32), 'wv': jax.random.normal(ks[3], (C, C), jnp.float32) * s, 'bv': jnp.zeros((C,), jnp.float32), 'wp': jax.random.normal(ks[4], (C, C), jnp.float32) * s, 'bp': jnp.zeros((C,), jnp.float32)}
        return inp
    _L0_conv_all = _L0_conv_setup()
    _L0_conv_in = {k: v for k, v in _L0_conv_all.items() if k in ('gamma', 'beta', 'wq', 'bq', 'wk', 'bk', 'wv', 'bv', 'wp', 'bp')}
    del _L0_conv_all

    def _L1_conv_setup():
        import jax, jax.numpy as jnp
        import numpy as np
        GROUPS = 32
        EPS = 1e-06
        key = jax.random.key(seed)
        ks = jax.random.split(key, 6)
        B, H, W, C = (4, 32, 32, 256)
        s = 1.0 / np.sqrt(C)
        return {'inputs': jax.random.normal(ks[0], (B, H, W, C), dtype=jnp.float32), 'gn_gamma': jnp.ones((C,), dtype=jnp.float32), 'gn_beta': jnp.zeros((C,), dtype=jnp.float32), 'wq': jax.random.normal(ks[1], (C, C), dtype=jnp.float32) * s, 'bq': jnp.zeros((C,), dtype=jnp.float32), 'wk': jax.random.normal(ks[2], (C, C), dtype=jnp.float32) * s, 'bk': jnp.zeros((C,), dtype=jnp.float32), 'wv': jax.random.normal(ks[3], (C, C), dtype=jnp.float32) * s, 'bv': jnp.zeros((C,), dtype=jnp.float32), 'wo': jax.random.normal(ks[4], (C, C), dtype=jnp.float32) * s, 'bo': jnp.zeros((C,), dtype=jnp.float32)}
    _L1_conv_all = _L1_conv_setup()
    _L1_conv_in = {k: v for k, v in _L1_conv_all.items() if k in ('gn_gamma', 'gn_beta', 'wq', 'bq', 'wk', 'bk', 'wv', 'bv', 'wo', 'bo')}
    del _L1_conv_all
    return {'x': x, 'L0_conv_gamma': _L0_conv_in['gamma'], 'L0_conv_beta': _L0_conv_in['beta'], 'L0_conv_wq': _L0_conv_in['wq'], 'L0_conv_bq': _L0_conv_in['bq'], 'L0_conv_wk': _L0_conv_in['wk'], 'L0_conv_bk': _L0_conv_in['bk'], 'L0_conv_wv': _L0_conv_in['wv'], 'L0_conv_bv': _L0_conv_in['bv'], 'L0_conv_wp': _L0_conv_in['wp'], 'L0_conv_bp': _L0_conv_in['bp'], 'L1_conv_gn_gamma': _L1_conv_in['gn_gamma'], 'L1_conv_gn_beta': _L1_conv_in['gn_beta'], 'L1_conv_wq': _L1_conv_in['wq'], 'L1_conv_bq': _L1_conv_in['bq'], 'L1_conv_wk': _L1_conv_in['wk'], 'L1_conv_bk': _L1_conv_in['bk'], 'L1_conv_wv': _L1_conv_in['wv'], 'L1_conv_bv': _L1_conv_in['bv'], 'L1_conv_wo': _L1_conv_in['wo'], 'L1_conv_bo': _L1_conv_in['bo']}

def reference(x, L0_conv_gamma, L0_conv_beta, L0_conv_wq, L0_conv_bq, L0_conv_wk, L0_conv_bk, L0_conv_wv, L0_conv_bv, L0_conv_wp, L0_conv_bp, L1_conv_gn_gamma, L1_conv_gn_beta, L1_conv_wq, L1_conv_bq, L1_conv_wk, L1_conv_bk, L1_conv_wv, L1_conv_bv, L1_conv_wo, L1_conv_bo):
    import jax
    import jax.numpy as jnp

    def _L0_conv_ref(x, gamma, beta, wq, bq, wk, bk, wv, bv, wp, bp):
        import jax, jax.numpy as jnp
        import numpy as np
        GROUPS = 32
        EPS = 1e-05

        def group_norm(x, gamma, beta):
            B, H, W, C = x.shape
            xg = x.reshape(B, H, W, GROUPS, C // GROUPS)
            mean = xg.mean(axis=(1, 2, 4), keepdims=True)
            var = xg.var(axis=(1, 2, 4), keepdims=True)
            xn = ((xg - mean) * jax.lax.rsqrt(var + EPS)).reshape(B, H, W, C)
            return xn * gamma + beta

        def conv1x1(x, w, b):
            return jnp.einsum('bhwc,cd->bhwd', x, w) + b
        B, H, W, C = x.shape
        N = H * W
        xn = group_norm(x, gamma, beta)
        q = conv1x1(xn, wq, bq).reshape(B, N, C)
        k = conv1x1(xn, wk, bk).reshape(B, N, C)
        v = conv1x1(xn, wv, bv).reshape(B, N, C)
        scale = 1.0 / jnp.sqrt(jnp.asarray(C, x.dtype))
        scores = jnp.einsum('bnc,bmc->bnm', q, k) * scale
        attn = jax.nn.softmax(scores, axis=-1)
        out = jnp.einsum('bnm,bmc->bnc', attn, v).reshape(B, H, W, C)
        return conv1x1(out, wp, bp) + x

    def _L1_conv_ref(inputs, gn_gamma, gn_beta, wq, bq, wk, bk, wv, bv, wo, bo):
        import jax, jax.numpy as jnp
        import numpy as np
        GROUPS = 32
        EPS = 1e-06
        B, H, W, C = inputs.shape
        xg = inputs.astype(jnp.float32).reshape(B, H, W, GROUPS, C // GROUPS)
        mean = jnp.mean(xg, axis=(1, 2, 4), keepdims=True)
        var = jnp.var(xg, axis=(1, 2, 4), keepdims=True)
        xg = (xg - mean) * jax.lax.rsqrt(var + EPS)
        x = xg.reshape(B, H, W, C) * gn_gamma + gn_beta
        q = jnp.einsum('bhwc,cd->bhwd', x, wq) + bq
        k = jnp.einsum('bhwc,cd->bhwd', x, wk) + bk
        v = jnp.einsum('bhwc,cd->bhwd', x, wv) + bv
        N = H * W
        q = q.reshape(B, N, C) * (1.0 / jnp.sqrt(jnp.float32(C)))
        k = k.reshape(B, N, C)
        v = v.reshape(B, N, C)
        scores = jnp.einsum('bnc,bmc->bnm', q, k)
        attn = jax.nn.softmax(scores.astype(jnp.float32), axis=-1).astype(q.dtype)
        out = jnp.einsum('bmc,bnm->bnc', v, attn)
        out = out.reshape(B, H, W, C)
        out = jnp.einsum('bhwc,cd->bhwd', out, wo) + bo
        return out + inputs

    def _gn(v, G=32, eps=1e-05):
        B_, H_, W_, C_ = v.shape
        g = v.reshape(B_, H_, W_, G, C_ // G)
        m = jnp.mean(g, axis=(1, 2, 4), keepdims=True)
        s = jnp.var(g, axis=(1, 2, 4), keepdims=True)
        return ((g - m) / jnp.sqrt(s + eps)).reshape(v.shape)

    def _ln_c(v, eps=1e-06):
        m = jnp.mean(v, axis=-1, keepdims=True)
        s = jnp.var(v, axis=-1, keepdims=True)
        return (v - m) / jnp.sqrt(s + eps)

    def _ln_t(v, eps=1e-05):
        m = jnp.mean(v, axis=-1, keepdims=True)
        s = jnp.var(v, axis=-1, keepdims=True)
        return (v - m) / jnp.sqrt(s + eps)

    def _to_tokens(v):
        B_, H_, W_, C_ = v.shape
        return v.reshape(B_, H_ * W_, C_)

    def _from_tokens(t, like):
        return t.reshape(like.shape)
    x = _L0_conv_ref(x, L0_conv_gamma, L0_conv_beta, L0_conv_wq, L0_conv_bq, L0_conv_wk, L0_conv_bk, L0_conv_wv, L0_conv_bv, L0_conv_wp, L0_conv_bp)
    x = _L1_conv_ref(x, L1_conv_gn_gamma, L1_conv_gn_beta, L1_conv_wq, L1_conv_bq, L1_conv_wk, L1_conv_bk, L1_conv_wv, L1_conv_bv, L1_conv_wo, L1_conv_bo)
    return x

_drawn_inputs = setup_inputs


def setup_inputs(seed=0):
    import zlib

    import numpy as np

    out = dict(_drawn_inputs(seed))
    spreads = {'L0_conv_gamma': (1.0, 0.2),
     'L0_conv_beta': (0.0, 0.1),
     'L0_conv_bq': (0.0, 0.66),
     'L0_conv_bk': (0.0, 0.8),
     'L0_conv_bv': (0.0, 0.1),
     'L0_conv_bp': (0.0, 0.1),
     'L1_conv_gn_gamma': (1.0, 0.2),
     'L1_conv_gn_beta': (0.0, 0.1),
     'L1_conv_bq': (0.0, 0.8),
     'L1_conv_bk': (0.0, 0.8),
     'L1_conv_bv': (0.0, 0.1),
     'L1_conv_bo': (0.0, 0.1)}
    factors = {}
    for name, (base, spread) in spreads.items():
        noise = np.random.default_rng([zlib.crc32(name.encode()), seed]).standard_normal(out[name].shape)
        drawn = base * np.exp(spread * noise) if base else spread * noise
        out[name] = jnp.asarray(drawn.astype(out[name].dtype))
    for name, factor in factors.items():
        out[name] = (out[name] * factor).astype(out[name].dtype)
    return out
```

```python
from contextlib import ExitStack

import concourse.bass as bass
from concourse import mybir

F32 = mybir.dt.float32
F32R = mybir.dt.float32r
ALU = mybir.AluOpType
ACT = mybir.ActivationFunctionType
AX_X = mybir.AxisListType.X

P = 128
GROUPS = 32
EPS = (1e-5, 1e-6)
BANK = 512
VECTORS = ("gamma", "beta", "bq", "bk", "bv")


def two_attention_layers(nc, x, layers, out):
    IMAGES, N, C = x.shape
    LAYERS = len(layers)
    UNITS = IMAGES * LAYERS
    KC = C // P
    NB = N // P
    HALVES = N // BANK
    BPH = NB // HALVES
    PER_GROUP = C // GROUPS
    WX = C + 2
    SCALE = 1.0 / 16.0
    NV = len(VECTORS)
    TQ = KC * HALVES
    assert C == 256 and N == 1024 and IMAGES == 2 and LAYERS == 2

    x_rows = x.rearrange("b (p k) c -> b p k c", k=NB)
    out_rows = out.rearrange("b (p k) c -> b p k c", k=NB)

    with ExitStack() as ctx:
        def sb(name, shape, dt=F32):
            return ctx.enter_context(nc.sbuf_tensor(name, shape, dt))

        def ps(name, shape):
            return ctx.enter_context(nc.psum_tensor(name, shape, F32))

        def sem(name):
            return ctx.enter_context(nc.semaphore(name))

        ident = sb("ident", [P, P])
        group_mean = sb("group_mean", [P, P])
        ones = sb("ones", [P, P])
        minus_half = sb("minus_half", [P, KC])
        xnat = sb("xnat", [P, IMAGES, NB, C])
        w_raw = {(l, k): sb(f"w_{k}{l}", [P, KC, C]) for l in range(LAYERS) for k in ("wq", "wk", "wv", "wp")}
        vec_rows = sb("vec_rows", [LAYERS * NV, C])
        vec_cols = sb("vec_cols", [P, KC, LAYERS * NV])
        bp_rows = sb("bp_rows", [1, LAYERS, C])
        bq_wide = sb("bq_wide", [P, LAYERS, KC, P])
        bv_wide = sb("bv_wide", [P, LAYERS, KC, P])
        wqT = sb("wqT", [P, LAYERS, KC, C])
        wkT_bk = sb("wkT_bk", [P, LAYERS, KC, C + 1])
        wvT = sb("wvT", [P, LAYERS, KC, C])
        A_hi = sb("A_hi", [P, LAYERS, KC, C], F32R)
        A_lo = sb("A_lo", [P, LAYERS, KC, C], F32R)
        Ac_hi = sb("Ac_hi", [P, KC, C], F32R)
        Ac_lo = sb("Ac_lo", [P, KC, C], F32R)
        Wx_hi = sb("Wx_hi", [P, LAYERS, KC, WX], F32R)
        Wx_lo = sb("Wx_lo", [P, LAYERS, KC, WX], F32R)
        NPAR = 3 * KC + 2
        G0, B0, U0, E0, D0 = 0, KC, 2 * KC, 3 * KC, 3 * KC + 1
        params = sb("params", [P, LAYERS, NPAR])
        par = sb("par", [P, NPAR])
        out_bias = sb("out_bias", [P, LAYERS, C])
        xstat = sb("xstat", [P, 2, C])
        xraw = sb("xraw", [P, KC, N])
        xn = sb("xn", [P, KC, N])
        xn_hi = sb("xn_hi", [P, KC, N], F32R)
        xn_lo = sb("xn_lo", [P, KC, N], F32R)
        t_hi = sb("t_hi", [P, KC, N], F32R)
        t_lo = sb("t_lo", [P, KC, N], F32R)
        tb_hi = sb("tb_hi", [P, 2, KC, P], F32R)
        tb_lo = sb("tb_lo", [P, 2, KC, P], F32R)
        V = sb("V", [P, NB, 2 * C], F32R)
        w_row = sb("w_row", [P, NB])
        probs = sb("probs", [P, 2, N])
        pT_hi = sb("pT_hi", [P, 2, NB, P], F32R)
        pT_lo = sb("pT_lo", [P, 2, NB, P], F32R)
        neg_max = sb("neg_max", [P, 2])
        exp_bias = sb("exp_bias", [P, 2])
        row_sum = sb("row_sum", [P, NB])
        row_inv = sb("row_inv", [P, 2])
        part_out = sb("part_out", [P, 2, C])
        bn = sb("bn", [P, KC, NB, 6])
        mv = sb("mv", [P, KC, 2])
        gmean = sb("gmean", [P, KC])
        dev = sb("dev", [P, KC])
        dev2 = sb("dev2", [P, KC])
        var_c = sb("var_c", [P, KC])
        var_e = sb("var_e", [P, KC])
        r0 = sb("r0", [P, KC])
        r0sq = sb("r0sq", [P, KC])
        r_err = sb("r_err", [P, KC])
        rstd = sb("rstd", [P, KC])
        gain = sb("gain", [P, KC])
        gain_mean = sb("gain_mean", [P, KC])
        shift = sb("shift", [P, KC])

        S = [ps(f"S{i}", [P, N]) for i in range(2)]
        T0 = ps("T0", [P, BANK])
        T1 = ps("T1", [P, BANK])
        O = ps("O", [P, BANK])
        X = ps("X", [P, BANK])
        PT = [T0, T1]
        T_RING = [T0, T1, O, X]
        V_RING = [T0, T1, O]

        ld_x = [[sem(f"ld_x{b}_{k}") for k in range(NB // 2)] for b in range(IMAGES)]
        ld_w = {(l, k): sem(f"ld_{k}{l}") for l in range(LAYERS) for k in ("wq", "wk", "wv", "wp")}
        ld_vec = sem("ld_vec")
        stored = sem("stored")
        po_const = sem("po_const")
        po_block = sem("po_block")
        po_xstat = sem("po_xstat")
        po_resid = sem("po_resid")
        po_unit = sem("po_unit")
        po_r0 = sem("po_r0")
        pe_vec = sem("pe_vec")
        pe_wT = sem("pe_wT")
        pe_A = sem("pe_A")
        pe_Wx = sem("pe_Wx")
        pe_small = sem("pe_small")
        pe_ob = sem("pe_ob")
        pe_xT = sem("pe_xT")
        pe_gm = sem("pe_gm")
        pe_gv = sem("pe_gv")
        pe_t = sem("pe_t")
        pe_S = sem("pe_S")
        pe_V = sem("pe_V")
        pe_pT = sem("pe_pT")
        pe_O = sem("pe_O")
        ac_wT = sem("ac_wT")
        ac_A = sem("ac_A")
        ac_Wx = sem("ac_Wx")
        ac_xT = sem("ac_xT")
        ac_t = sem("ac_t")
        ac_V = sem("ac_V")
        ac_P = sem("ac_P")
        ac_pT = sem("ac_pT")
        ac_xh = sem("ac_xh")
        dv_const = sem("dv_const")
        dv_vec = sem("dv_vec")
        dv_wide = sem("dv_wide")
        dv_wT = sem("dv_wT")
        dv_A = sem("dv_A")
        dv_Wx = sem("dv_Wx")
        dv_small = sem("dv_small")
        dv_ob = sem("dv_ob")
        dv_bn = sem("dv_bn")
        dv_stat = sem("dv_stat")
        dv_t = sem("dv_t")
        dv_V = sem("dv_V")
        dv_max = sem("dv_max")
        dv_bias = sem("dv_bias")
        dv_pT = sem("dv_pT")
        dv_inv = sem("dv_inv")
        dv_part = sem("dv_part")
        dv_O = sem("dv_O")
        dv_xn = sem("dv_xn")
        dv_xl = sem("dv_xl")
        FIRST = 1
        AGGR, DEV, DEV2, VARC, VARE, R0SQ, RERR, RSTD, GAIN, GMUL, SHIFT = range(1, 12)
        STAT = SHIFT


        block = ctx.enter_context(nc.Block())

        @block.sync
        def _(sp):
            for k in range(NB // 2):
                sp.dma_start(xnat[:, 0, 2 * k:2 * k + 2, :], x_rows[0, :, 2 * k:2 * k + 2, :]).then_inc(ld_x[0][k], 16)
            for l in range(LAYERS):
                for name in ("wq", "wk", "wv", "wp"):
                    sp.dma_start(w_raw[l, name][:], layers[l][name].rearrange("(k p) d -> p k d", p=P)
                                 ).then_inc(ld_w[l, name], 16)
                if l == 0:
                    for k in range(NB // 2):
                        sp.dma_start(xnat[:, 1, 2 * k:2 * k + 2, :], x_rows[1, :, 2 * k:2 * k + 2, :]
                                     ).then_inc(ld_x[1][k], 16)
            with sp.Fori(0, IMAGES) as b:
                for i in range(NB):
                    sp.wait_ge(dv_O, FIRST + b * NB + (UNITS - IMAGES) * NB + i + 1)
                    sp.dma_start(out_rows[bass.ds(b, 1), :, i:i + 1, :], xnat[:, bass.ds(b, 1), i:i + 1, :]
                                 ).then_inc(stored, 16)
            sp.wait_ge(stored, 16 * IMAGES * NB)

        @block.gpsimd
        def _(pool):
            nc.gpsimd.memset(ident[:], 1.0).then_inc(po_const, 1)
            nc.gpsimd.memset(group_mean[:], 1.0 / PER_GROUP).then_inc(po_const, 1)
            pool.wait_ge(po_const, 2)
            nc.gpsimd.affine_select(out=ident[:], in_=ident[:], compare_op=ALU.is_equal, fill=0.0, base=0,
                                    pattern=[[-1, P]], channel_multiplier=1).then_inc(po_const, 1)
            gv = group_mean[:, :].rearrange("p (g j) -> p g j", j=PER_GROUP)
            nc.gpsimd.affine_select(out=gv, in_=gv, compare_op=ALU.is_ge, fill=0.0, base=0,
                                    pattern=[[-PER_GROUP, P // PER_GROUP], [0, PER_GROUP]],
                                    channel_multiplier=1).then_inc(po_const, 1)
            pool.wait_ge(po_const, 4)
            nc.gpsimd.affine_select(out=gv, in_=gv, compare_op=ALU.is_ge, fill=0.0, base=PER_GROUP - 1,
                                    pattern=[[PER_GROUP, P // PER_GROUP], [0, PER_GROUP]],
                                    channel_multiplier=-1).then_inc(po_const, 1)

            def unit_constants(v, l):
                nc.gpsimd.tensor_copy(Ac_hi[:], A_hi[:, l]).then_inc(po_unit, 1)
                nc.gpsimd.tensor_copy(Ac_lo[:], A_lo[:, l]).then_inc(po_unit, 1)
                nc.gpsimd.tensor_copy(par[:], params[:, l]).then_inc(po_unit, 1)

            def power(v):
                pool.wait_ge(dv_stat, v * STAT + VARE)
                nc.gpsimd.tensor_tensor(r0[:], var_e[:], minus_half[:], ALU.pow).then_inc(po_r0, 1)

            pool.wait_ge(dv_A, KC)
            pool.wait_ge(dv_small, 1)
            pool.wait_ge(dv_const, 1)
            nc.gpsimd.tensor_copy(Ac_hi[:], A_hi[:, 0]).then_inc(po_unit, 1)
            nc.gpsimd.tensor_copy(Ac_lo[:], A_lo[:, 0]).then_inc(po_unit, 1)
            nc.gpsimd.tensor_copy(par[:], params[:, 0]).then_inc(po_unit, 1)
            power(0)
            pool.wait_ge(pe_xT, NB)
            pool.wait_ge(dv_ob, LAYERS)
            pool.wait_ge(dv_A, LAYERS * KC)
            for k in range(NB // 2):
                pool.wait_ge(ld_x[1][k], 16)

            def t_block(u, i, parity):
                for src, dst in ((t_hi, tb_hi), (t_lo, tb_lo)):
                    nc.gpsimd.tensor_copy(dst[:, parity], src[:, :, bass.ds(i * P, P)]).then_inc(po_block, 1)

            def next_rows(u, i, parity):
                nc.gpsimd.tensor_copy(xstat[:, parity:parity + 1, :], xnat[:, bass.ds((u + 1) % IMAGES, 1), bass.ds(i, 1), :]
                                      .rearrange("p a b c -> p (a b) c")).then_inc(po_xstat, 1)

            def residual(u, i):
                rows = xnat[:, bass.ds(u % IMAGES, 1), bass.ds(i, 1), :].rearrange("p a b c -> p (a b) c")
                nc.gpsimd.tensor_tensor(rows, rows, out_bias[:, bass.ds(u // IMAGES, 1), :], ALU.add).then_inc(po_resid, 1)

            def unit(u, last):
                pool.wait_ge(dv_t, u * TQ + KC)
                pool.wait_ge(dv_O, FIRST + u * NB)
                residual(u, 0)
                for i in range(2):
                    t_block(u, i, i)
                residual(u, 1)
                if not last:
                    for i in range(2):
                        next_rows(u, i, i)
                with pool.Fori(0, NB // 2 - 1) as j:
                    for k in range(2):
                        i = 2 * j + k
                        pool.wait_ge(dv_t, u * TQ + TQ)
                        pool.wait_ge(pe_S, u * NB + i + 1)
                        t_block(u, i + 2, k)
                        if not last:
                            pool.wait_ge(pe_xT, u * NB + NB + i + 1)
                            next_rows(u, i + 2, k)
                        residual(u, i + 2)
                if not last:
                    pool.wait_ge(dv_V, u * NB + NB)
                    l = (u + 1) // IMAGES
                    nc.gpsimd.tensor_copy(Ac_hi[:], A_hi[:, bass.ds(l, 1)].rearrange("p a k c -> p (a k) c")).then_inc(po_unit, 1)
                    nc.gpsimd.tensor_copy(Ac_lo[:], A_lo[:, bass.ds(l, 1)].rearrange("p a k c -> p (a k) c")).then_inc(po_unit, 1)
                    nc.gpsimd.tensor_copy(par[:], params[:, bass.ds(l, 1), :].rearrange("p a n -> p (a n)")).then_inc(po_unit, 1)
                    power(u + 1)

            with pool.Fori(0, UNITS - 1) as u:
                unit(u, False)
            unit(UNITS - 1, True)

        @block.scalar
        def _(act):
            for l in range(LAYERS):
                for n, name in enumerate(VECTORS):
                    r = l * NV + n
                    act.dma_start(vec_rows[r:r + 1, :], layers[l][name].rearrange("(a c) -> a c", a=1)).then_inc(ld_vec, 16)
                act.dma_start(bp_rows[0:1, l, :], layers[l]["bp"].rearrange("(a c) -> a c", a=1)).then_inc(ld_vec, 16)

            def raw_rows(v, i):
                act.wait_ge(pe_xT, v * NB + i + 1)
                nc.scalar.copy(xraw[:, :, bass.ds(i * P, P)],
                               X[:, 0:KC * P].rearrange("p (k n) -> p k n", k=KC)).then_inc(ac_xT, 1)

            def weights(l):
                act.wait_ge(pe_wT, 3 * l + 1)
                nc.scalar.copy(wqT[:, l], T0[:, :].rearrange("p (k c) -> p k c", k=KC)).then_inc(ac_wT, 1)
                act.wait_ge(pe_wT, 3 * l + 3)
                nc.scalar.copy(wvT[:, l], O[:, :].rearrange("p (k c) -> p k c", k=KC)).then_inc(ac_wT, 1)
                for k in range(KC):
                    act.wait_ge(pe_A, KC * l + k + 1)
                    nc.scalar.activation(A_hi[:, l, k, :], S[0][:, k * BANK:k * BANK + C], ACT.Identity, scale=SCALE)
                    nc.scalar.activation(Wx_hi[:, l, k, C:C + 1], S[0][:, k * BANK + C:k * BANK + C + 1],
                                         ACT.Identity, scale=SCALE).then_inc(ac_A, 1)
                for k in range(KC):
                    act.wait_ge(pe_Wx, KC * l + k + 1)
                    nc.scalar.copy(Wx_hi[:, l, k, 0:C], S[1][:, k * BANK:k * BANK + C]).then_inc(ac_Wx, 1)

            def xn_high(v):
                act.wait_ge(dv_stat, v * STAT + SHIFT)
                for k in range(KC):
                    nc.scalar.activation(xn_hi[:, k, :], xraw[:, k, :], ACT.Identity, scale=gain[:, k:k + 1],
                                         bias=shift[:, k:k + 1]).then_inc(ac_xh, 1)

            for i in range(NB):
                raw_rows(0, i)
            weights(0)
            xn_high(0)
            weights(1)

            def v_high(u, m):
                act.wait_ge(pe_V, u * NB + m + 1)
                nc.scalar.copy(V[:, m, 0:C], V_RING[m % 3][:, 0:C]).then_inc(ac_V, 1)

            def exponentials(u, i, parity):
                act.wait_ge(dv_bias, u * NB + i + 1)
                nc.scalar.activation(probs[:, parity, :], S[parity][:], ACT.Exp, bias=exp_bias[:, parity:parity + 1],
                                     accum_out=row_sum[:, bass.ds(i, 1)]).then_inc(ac_P, 1)

            def p_high(u, i, parity):
                for h in range(HALVES):
                    act.wait_ge(pe_pT, (u * NB + i) * HALVES + h + 1)
                    nc.scalar.copy(pT_hi[:, parity, h * BPH:(h + 1) * BPH, :],
                                   PT[h][:, :].rearrange("p (m n) -> p m n", m=BPH)).then_inc(ac_pT, 1)

            def unit(u, last):
                for q in range(TQ):
                    h, k = divmod(q, KC)
                    act.wait_ge(pe_t, u * TQ + q + 1)
                    nc.scalar.activation(t_hi[:, k, h * BANK:(h + 1) * BANK], T_RING[q][:], ACT.Identity,
                                         bias=par[:, U0 + k:U0 + k + 1]).then_inc(ac_t, 1)
                v_high(u, 0)
                exponentials(u, 0, 0)
                for m in range(1, 4):
                    v_high(u, m)
                if not last:
                    raw_rows(u + 1, 0)
                v_high(u, 4)
                exponentials(u, 1, 1)
                for m in range(5, 8):
                    v_high(u, m)
                if not last:
                    raw_rows(u + 1, 1)
                p_high(u, 0, 0)
                with act.Fori(0, NB // 2 - 1) as j:
                    for k in range(2):
                        i = 2 * j + k
                        if not last:
                            raw_rows(u + 1, i + 2)
                        p_high(u, i + 1, 1 - k)
                        exponentials(u, i + 2, k)
                p_high(u, NB - 1, 1)
                if not last:
                    xn_high(u + 1)

            with act.Fori(0, UNITS - 1) as u:
                unit(u, False)
            unit(UNITS - 1, True)

        @block.vector
        def _(dve):
            nc.vector.memset(ones[:], 1.0).then_inc(dv_O, FIRST)
            nc.vector.memset(minus_half[:], -0.5)
            for l in range(LAYERS):
                nc.vector.memset(params[:, l, E0:E0 + 1], EPS[l])
                for wx in (Wx_hi, Wx_lo):
                    last = nc.vector.memset(wx[:, l, :, C + 1:WX].bitcast(F32), 0.0)
            last.then_inc(dv_const, 1)
            dve.wait_ge(dv_const, 1)

            def statistics_of(v, i):
                dve.wait_ge(ac_xT, v * NB + i + 1)
                for k in range(KC):
                    last = nc.vector.bn_stats(bn[:, k:k + 1, bass.ds(i, 1), :].rearrange("p a b s -> p (a b s)"),
                                              xraw[:, k, bass.ds(i * P, P)])
                last.then_inc(dv_bn, 1)

            def vectors():
                dve.wait_ge(pe_vec, 1)
                nc.vector.tensor_copy(vec_cols[:], X[:, 0:KC * LAYERS * NV].rearrange("p (k r) -> p k r", k=KC)
                                      ).then_inc(dv_vec, 1)
                dve.wait_ge(dv_vec, 1)
                for l in range(LAYERS):
                    for n, at in (("gamma", G0), ("beta", B0)):
                        nc.vector.tensor_copy(params[:, l, at:at + KC], vec_cols[:, :, l * NV + VECTORS.index(n)])
                    nc.vector.tensor_copy(wkT_bk[:, l, :, C], vec_cols[:, :, l * NV + VECTORS.index("bk")])
                    for n, wide in (("bq", bq_wide), ("bv", bv_wide)):
                        r = l * NV + VECTORS.index(n)
                        for k in range(KC):
                            last = nc.vector.tensor_scalar(wide[:, l, k, :], ones[:], vec_cols[:, k, r:r + 1], None, ALU.mult)
                    last.then_inc(dv_wide, 1)

            def weights(l):
                dve.wait_ge(pe_wT, 3 * l + 2)
                nc.vector.tensor_copy(wkT_bk[:, l, :, 0:C], T1[:, :].rearrange("p (k c) -> p k c", k=KC)).then_inc(dv_wT, 1)
                for k in range(KC):
                    dve.wait_ge(ac_A, KC * l + k + 1)
                    nc.vector.scalar_tensor_tensor(A_lo[:, l, k, :], S[0][:, k * BANK:k * BANK + C], SCALE,
                                                   A_hi[:, l, k, :].bitcast(F32), ALU.mult, ALU.subtract)
                    nc.vector.scalar_tensor_tensor(Wx_lo[:, l, k, C:C + 1], S[0][:, k * BANK + C:k * BANK + C + 1], SCALE,
                                                   Wx_hi[:, l, k, C:C + 1].bitcast(F32), ALU.mult, ALU.subtract
                                                   ).then_inc(dv_A, 1)
                for k in range(KC):
                    dve.wait_ge(ac_Wx, KC * l + k + 1)
                    nc.vector.tensor_tensor(Wx_lo[:, l, k, 0:C], S[1][:, k * BANK:k * BANK + C],
                                            Wx_hi[:, l, k, 0:C].bitcast(F32), ALU.subtract).then_inc(dv_Wx, 1)
                dve.wait_ge(pe_small, l + 1)
                nc.vector.tensor_scalar(params[:, l, U0:U0 + KC], T1[:, 0:KC], SCALE, None, ALU.mult)
                nc.vector.tensor_scalar(params[:, l, D0:D0 + 1], T1[:, KC:KC + 1], SCALE, None, ALU.mult).then_inc(dv_small, 1)
                dve.wait_ge(pe_ob, l + 1)
                nc.vector.tensor_copy(out_bias[:, l, :], T0[:, 0:C]).then_inc(dv_ob, 1)

            def group_statistics(v):
                at = v * STAT
                for k in range(KC):
                    last = nc.vector.bn_aggr(mv[:, k, :], bn[:, k, :, :].rearrange("p b s -> p (b s)"))
                last.then_inc(dv_stat, 1)
                dve.wait_ge(pe_gm, v + 1)
                nc.vector.tensor_copy(gmean[:], X[:, 0:KC])
                dve.wait_ge(dv_stat, at + AGGR)
                nc.vector.tensor_tensor(dev[:], mv[:, :, 0], X[:, 0:KC], ALU.subtract).then_inc(dv_stat, 1)
                dve.wait_ge(dv_stat, at + DEV)
                nc.vector.tensor_tensor(dev2[:], dev[:], dev[:], ALU.mult).then_inc(dv_stat, 1)
                dve.wait_ge(dv_stat, at + DEV2)
                nc.vector.tensor_tensor(var_c[:], dev2[:], mv[:, :, 1], ALU.add).then_inc(dv_stat, 1)

            def affine_map(v):
                at = v * STAT
                dve.wait_ge(pe_gv, v + 1)
                dve.wait_ge(po_unit, v * 3 + 3)
                nc.vector.tensor_scalar(var_e[:], X[:, 0:KC], par[:, E0:E0 + 1], None, ALU.add).then_inc(dv_stat, 1)
                dve.wait_ge(po_r0, v + 1)
                nc.vector.tensor_tensor(r0sq[:], r0[:], r0[:], ALU.mult).then_inc(dv_stat, 1)
                dve.wait_ge(dv_stat, at + R0SQ)
                nc.vector.scalar_tensor_tensor(r_err[:], r0sq[:], -0.5, var_e[:], ALU.mult, ALU.mult).then_inc(dv_stat, 1)
                dve.wait_ge(dv_stat, at + RERR)
                nc.vector.scalar_tensor_tensor(rstd[:], r_err[:], 1.5, r0[:], ALU.add, ALU.mult).then_inc(dv_stat, 1)
                dve.wait_ge(dv_stat, at + RSTD)
                nc.vector.tensor_tensor(gain[:], rstd[:], par[:, G0:G0 + KC], ALU.mult).then_inc(dv_stat, 1)
                dve.wait_ge(dv_stat, at + GAIN)
                nc.vector.tensor_tensor(gain_mean[:], gain[:], gmean[:], ALU.mult).then_inc(dv_stat, 1)
                dve.wait_ge(dv_stat, at + GMUL)
                nc.vector.tensor_tensor(shift[:], par[:, B0:B0 + KC], gain_mean[:], ALU.subtract).then_inc(dv_stat, 1)

            def normalise(v):
                dve.wait_ge(dv_stat, v * STAT + SHIFT)
                for k in range(KC):
                    nc.vector.tensor_scalar(xn[:, k, :], xraw[:, k, :], gain[:, k:k + 1], shift[:, k:k + 1],
                                            ALU.mult, ALU.add).then_inc(dv_xn, 1)

            def xn_low(v):
                for k in range(KC):
                    dve.wait_ge(dv_xn, v * KC + k + 1)
                    dve.wait_ge(ac_xh, v * KC + k + 1)
                    nc.vector.tensor_tensor(xn_lo[:, k, :], xn[:, k, :], xn_hi[:, k, :].bitcast(F32),
                                            ALU.subtract).then_inc(dv_xl, 1)

            vectors()
            for i in range(NB):
                statistics_of(0, i)
            dve.wait_ge(dv_bn, NB)
            group_statistics(0)
            weights(0)
            affine_map(0)
            normalise(0)
            xn_low(0)
            weights(1)

            def v_low(u, m):
                bank = V_RING[m % 3]
                dve.wait_ge(ac_V, u * NB + m + 1)
                nc.vector.tensor_tensor(V[:, m, C:2 * C], bank[:, 0:C], V[:, m, 0:C].bitcast(F32), ALU.subtract)
                nc.vector.tensor_scalar(w_row[:, m:m + 1], bank[:, C:C + 1], par[:, D0:D0 + 1], None, ALU.add
                                        ).then_inc(dv_V, 1)

            def row_max(u, i, parity):
                dve.wait_ge(pe_S, u * NB + i + 1)
                nc.vector.tensor_reduce(neg_max[:, parity:parity + 1], S[parity][:], AX_X, ALU.max, negate=True
                                        ).then_inc(dv_max, 1)

            def bias_of(u, i, parity, first=False):
                dve.wait_ge(dv_V, u * NB + (i + 1 if first else NB))
                dve.wait_ge(dv_max, u * NB + i + 1)
                w = w_row[:, bass.ds(i, 1)]
                nc.vector.scalar_tensor_tensor(exp_bias[:, parity:parity + 1], neg_max[:, parity:parity + 1], w, w,
                                               ALU.subtract, ALU.add).then_inc(dv_bias, 1)

            def p_low(u, i, parity):
                for h in range(HALVES):
                    dve.wait_ge(ac_pT, (u * NB + i) * HALVES + h + 1)
                    nc.vector.tensor_tensor(pT_lo[:, parity, h * BPH:(h + 1) * BPH, :],
                                            PT[h][:, :].rearrange("p (m n) -> p m n", m=BPH),
                                            pT_hi[:, parity, h * BPH:(h + 1) * BPH, :].bitcast(F32),
                                            ALU.subtract).then_inc(dv_pT, 1)

            def output(u, i, parity, bank):
                nc.vector.reciprocal(row_inv[:, parity:parity + 1], row_sum[:, bass.ds(i, 1)]).then_inc(dv_inv, 1)
                dve.wait_ge(dv_inv, u * NB + i + 1)
                dve.wait_ge(pe_O, u * NB + i + 1)
                dve.wait_ge(po_resid, u * NB + i + 1)
                rows = xnat[:, bass.ds(u % IMAGES, 1), bass.ds(i, 1), :].rearrange("p a b c -> p (a b c)")
                inv = row_inv[:, parity:parity + 1]
                nc.vector.scalar_tensor_tensor(part_out[:, parity, :], bank[:, C:2 * C], inv, rows,
                                               ALU.mult, ALU.add).then_inc(dv_part, 1)
                dve.wait_ge(dv_part, u * NB + i + 1)
                nc.vector.scalar_tensor_tensor(rows, bank[:, 0:C], inv, part_out[:, parity, :],
                                               ALU.mult, ALU.add).then_inc(dv_O, 1)

            def unit(u, last):
                for q in range(TQ):
                    h, k = divmod(q, KC)
                    dve.wait_ge(ac_t, u * TQ + q + 1)
                    cols = slice(h * BANK, (h + 1) * BANK)
                    nc.vector.scalar_tensor_tensor(t_lo[:, k, cols], T_RING[q][:], par[:, U0 + k:U0 + k + 1],
                                                   t_hi[:, k, cols].bitcast(F32), ALU.add, ALU.subtract
                                                   ).then_inc(dv_t, 1)
                row_max(u, 0, 0)
                v_low(u, 0)
                bias_of(u, 0, 0, first=True)
                for m in range(1, 4):
                    v_low(u, m)
                row_max(u, 1, 1)
                v_low(u, 4)
                bias_of(u, 1, 1, first=True)
                for m in range(5, 8):
                    v_low(u, m)
                if not last:
                    statistics_of(u + 1, 0)
                    statistics_of(u + 1, 1)
                p_low(u, 0, 0)
                with dve.Fori(0, NB // 2 - 1) as j:
                    for k in range(2):
                        i = 2 * j + k
                        if not last:
                            statistics_of(u + 1, i + 2)
                            dve.wait_ge(dv_bn, u * NB + NB + i + 3)
                        row_max(u, i + 2, k)
                        bias_of(u, i + 2, k)
                        p_low(u, i + 1, 1 - k)
                        output(u, i, k, O)
                if not last:
                    group_statistics(u + 1)
                p_low(u, NB - 1, 1)
                if not last:
                    affine_map(u + 1)
                    normalise(u + 1)
                output(u, NB - 2, 0, O)
                if not last:
                    xn_low(u + 1)
                output(u, NB - 1, 1, X)

            with dve.Fori(0, UNITS - 1) as u:
                unit(u, False)
            unit(UNITS - 1, True)

        @block.tensor
        def _(pe):
            def passes(bank, pairs, start=True):
                todo = [(lo_s, hi_m) for (_, lo_s), (hi_m, _) in pairs]
                todo += [p for (hi_s, _), (hi_m, lo_m) in pairs for p in ((hi_s, lo_m), (hi_s, hi_m))]
                for n, (stationary, moving) in enumerate(todo):
                    last = nc.tensor.matmul(bank, stationary, moving, start=(n == 0), stop=(n == len(todo) - 1))
                return last

            def weights(l):
                for n, (name, bank) in enumerate((("wq", T0), ("wk", T1), ("wv", O))):
                    pe.wait_ge(ld_w[l, name], 16)
                    if l:
                        pe.wait_ge(*((dv_ob, 1), (dv_small, 1), (ac_wT, 2))[n])
                    for kd in range(KC):
                        for kc in range(KC):
                            last = nc.tensor.transpose(bank[:, kd * C + kc * P:kd * C + (kc + 1) * P],
                                                       w_raw[l, name][:, kc, kd * P:(kd + 1) * P], ident[:])
                    last.then_inc(pe_wT, 1)
                pe.wait_ge(ac_wT, 2 * l + 1)
                pe.wait_ge(dv_wT, l + 1)
                pe.wait_ge(dv_wide, l + 1)
                for mc in range(KC):
                    if l:
                        pe.wait_ge(dv_A, mc + 1)
                    for kd in range(KC):
                        last = nc.tensor.matmul(S[0][:, mc * BANK:mc * BANK + C + 1], wqT[:, l, kd, mc * P:(mc + 1) * P],
                                                wkT_bk[:, l, kd, :], start=(kd == 0), stop=(kd == KC - 1))
                    last.then_inc(pe_A, 1)
                pe.wait_ge(ac_wT, 2 * l + 2)
                pe.wait_ge(ld_w[l, "wp"], 16)
                for mc in range(KC):
                    if l:
                        pe.wait_ge(dv_Wx, mc + 1)
                    for kd in range(KC):
                        last = nc.tensor.matmul(S[1][:, mc * BANK:mc * BANK + C], wvT[:, l, kd, mc * P:(mc + 1) * P],
                                                w_raw[l, "wp"][:, kd, :], start=(kd == 0), stop=(kd == KC - 1))
                    last.then_inc(pe_Wx, 1)
                for mc in range(KC):
                    for kd in range(KC):
                        r = l * NV + VECTORS.index("bq")
                        nc.tensor.matmul(T1[:, mc:mc + 1], wkT_bk[:, l, kd, mc * P:(mc + 1) * P],
                                         vec_cols[:, kd, r:r + 1], start=(kd == 0), stop=(kd == KC - 1))
                for kd in range(KC):
                    r = l * NV + VECTORS.index("bk")
                    last = nc.tensor.matmul(T1[:, KC:KC + 1], bq_wide[:, l, kd, :], vec_cols[:, kd, r:r + 1],
                                            start=(kd == 0), stop=(kd == KC - 1))
                last.then_inc(pe_small, 1)
                nc.tensor.matmul(T0[:, 0:C], ones[0:1, :], bp_rows[0:1, l, :], start=True, stop=False)
                for kd in range(KC):
                    last = nc.tensor.matmul(T0[:, 0:C], bv_wide[:, l, kd, :], w_raw[l, "wp"][:, kd, :],
                                            start=False, stop=(kd == KC - 1))
                last.then_inc(pe_ob, 1)

            def transpose_rows(block_of_rows):
                for k in range(KC):
                    last = nc.tensor.transpose(X[:, k * P:(k + 1) * P], block_of_rows(k), ident[:])
                last.then_inc(pe_xT, 1)

            def mean_of_groups(v):
                pe.wait_ge(ac_xT, v * NB + NB)
                pe.wait_ge(dv_stat, v * STAT + AGGR)
                nc.tensor.matmul(X[:, 0:KC], group_mean[:], mv[:, :, 0], start=True, stop=True).then_inc(pe_gm, 1)

            def variance_of_groups(v):
                pe.wait_ge(dv_stat, v * STAT + VARC)
                nc.tensor.matmul(X[:, 0:KC], group_mean[:], var_c[:], start=True, stop=True).then_inc(pe_gv, 1)

            pe.wait_ge(po_const, 5)
            pe.wait_ge(ld_vec, 16 * LAYERS * (NV + 1))
            for k in range(KC):
                last = nc.tensor.transpose(X[:, k * LAYERS * NV:(k + 1) * LAYERS * NV], vec_rows[:, k * P:(k + 1) * P],
                                           ident[0:LAYERS * NV, 0:LAYERS * NV])
            last.then_inc(pe_vec, 1)
            pe.wait_ge(dv_vec, 1)
            for i in range(NB):
                pe.wait_ge(ld_x[0][i // 2], 16)
                if i:
                    pe.wait_ge(ac_xT, i)
                transpose_rows(lambda k: xnat[:, 0, i, k * P:(k + 1) * P])
            mean_of_groups(0)
            variance_of_groups(0)
            weights(0)
            weights(1)
            pe.wait_ge(dv_ob, LAYERS)
            pe.wait_ge(dv_Wx, LAYERS * KC)

            def t_product(u):
                pe.wait_ge(po_unit, u * 3 + 3)
                pe.wait_ge(dv_xl, u * KC + KC)
                for q in range(TQ):
                    h, k = divmod(q, KC)
                    cols = slice(h * BANK, (h + 1) * BANK)
                    if q == 2:
                        pe.wait_ge(dv_O, FIRST + u * NB)
                    if q == 3:
                        pe.wait_ge(dv_stat, u * STAT + SHIFT)
                    passes(T_RING[q][:], [((Ac_hi[:, kc, k * P:(k + 1) * P], Ac_lo[:, kc, k * P:(k + 1) * P]),
                                           (xn_hi[:, kc, cols], xn_lo[:, kc, cols])) for kc in range(KC)]
                           ).then_inc(pe_t, 1)

            def scores(u, i, parity, first=False):
                pe.wait_ge(po_block, (u * NB + i) * 2 + 2)
                if not first:
                    pe.wait_ge(ac_P, u * NB + i - 1)
                todo = []
                for kc in range(KC):
                    todo.append((tb_lo[:, parity, kc, :], xn_hi, kc))
                    todo.append((tb_hi[:, parity, kc, :], xn_lo, kc))
                    todo.append((tb_hi[:, parity, kc, :], xn_hi, kc))
                for n, (stationary, moving, kc) in enumerate(todo):
                    for h in range(HALVES):
                        last = nc.tensor.matmul(S[parity][:, h * BANK:(h + 1) * BANK], stationary,
                                                moving[:, kc, h * BANK:(h + 1) * BANK],
                                                start=(n == 0), stop=(n == len(todo) - 1))
                last.then_inc(pe_S, 1)

            def values(u, m):
                if m < 3:
                    pe.wait_ge(dv_t, u * TQ + m + 1)
                else:
                    pe.wait_ge(dv_V, u * NB + m - 2)
                rows = slice(m * P, (m + 1) * P)
                l = bass.ds(u // IMAGES, 1)
                passes(V_RING[m % 3][:, 0:WX], [((xn_hi[:, kc, rows], xn_lo[:, kc, rows]),
                                                 (Wx_hi[:, l, kc, :].rearrange("p a c -> p (a c)"),
                                                  Wx_lo[:, l, kc, :].rearrange("p a c -> p (a c)")))
                                                for kc in range(KC)]).then_inc(pe_V, 1)

            def next_rows(u, i, parity, first=False):
                pe.wait_ge(po_xstat, u * NB + i + 1)
                if first:
                    pe.wait_ge(dv_t, u * TQ + TQ)
                else:
                    pe.wait_ge(ac_xT, u * NB + NB + i)
                transpose_rows(lambda k: xstat[:, parity, k * P:(k + 1) * P])

            def transpose_probs(u, i, parity, first=False):
                pe.wait_ge(ac_P, u * NB + i + 1)
                if first:
                    pe.wait_ge(dv_V, u * NB + NB)
                else:
                    pe.wait_ge(dv_pT, (u * NB + i) * HALVES)
                for h in range(HALVES):
                    for m in range(BPH):
                        at = (h * BPH + m) * P
                        last = nc.tensor.transpose(PT[h][:, m * P:(m + 1) * P], probs[:, parity, at:at + P], ident[:])
                    last.then_inc(pe_pT, 1)

            def attend(u, i, parity, bank):
                pe.wait_ge(dv_pT, (u * NB + i) * HALVES + HALVES)
                for m in range(NB):
                    nc.tensor.matmul(bank[:], pT_hi[:, parity, m, :], V[:, m, :], start=(m == 0), stop=False)
                    last = nc.tensor.matmul(bank[:, C:2 * C], pT_lo[:, parity, m, :], V[:, m, 0:C],
                                            start=False, stop=(m == NB - 1))
                last.then_inc(pe_O, 1)

            def unit(u, last):
                t_product(u)
                scores(u, 0, 0, first=True)
                for m in range(0, 4):
                    values(u, m)
                if not last:
                    next_rows(u, 0, 0, first=True)
                scores(u, 1, 1, first=True)
                for m in range(4, 8):
                    values(u, m)
                if not last:
                    next_rows(u, 1, 1)
                transpose_probs(u, 0, 0, first=True)
                with pe.Fori(0, NB // 2 - 1) as j:
                    for k in range(2):
                        i = 2 * j + k
                        if not last:
                            next_rows(u, i + 2, k)
                        scores(u, i + 2, k)
                        transpose_probs(u, i + 1, 1 - k)
                        pe.wait_ge(dv_O, FIRST + u * NB + i)
                        attend(u, i, k, O)
                if not last:
                    mean_of_groups(u + 1)
                transpose_probs(u, NB - 1, 1)
                if not last:
                    variance_of_groups(u + 1)
                pe.wait_ge(dv_O, FIRST + u * NB + NB - 2)
                attend(u, NB - 2, 0, O)
                if not last:
                    pe.wait_ge(dv_stat, (u + 1) * STAT + VARE)
                attend(u, NB - 1, 1, X)

            with pe.Fori(0, UNITS - 1) as u:
                unit(u, False)
            unit(UNITS - 1, True)


_L0 = {"gamma": "L0_conv_gamma", "beta": "L0_conv_beta", "wq": "L0_conv_wq", "bq": "L0_conv_bq", "wk": "L0_conv_wk",
       "bk": "L0_conv_bk", "wv": "L0_conv_wv", "bv": "L0_conv_bv", "wp": "L0_conv_wp", "bp": "L0_conv_bp"}
_L1 = {"gamma": "L1_conv_gn_gamma", "beta": "L1_conv_gn_beta", "wq": "L1_conv_wq", "bq": "L1_conv_bq",
       "wk": "L1_conv_wk", "bk": "L1_conv_bk", "wv": "L1_conv_wv", "bv": "L1_conv_bv", "wp": "L1_conv_wo",
       "bp": "L1_conv_bo"}


def kernel(**inputs):
    import numpy as _np
    import concourse.bacc as _bacc
    from concourse import mybir as _mybir
    from concourse.bass_utils import run_bass_kernel_spmd as _run

    nc = _bacc.Bacc("TRN2", target_bir_lowering=False, num_devices=1)
    arrays = {}

    def dram(name):
        a = _np.ascontiguousarray(inputs[name])
        arrays[f"in_{name}"] = a
        return nc.dram_tensor(f"in_{name}", a.shape, _mybir.dt.from_np(a.dtype), kind="ExternalInput").ap()

    x = dram("x")
    layers = [{k: dram(n) for k, n in names.items()} for names in (_L0, _L1)]
    shape = inputs["x"].shape
    out = nc.dram_tensor("out_0", shape, _mybir.dt.float32, kind="ExternalOutput").ap()
    two_attention_layers(nc, x.rearrange("b h w c -> b (h w) c"), layers, out.rearrange("b h w c -> b (h w) c"))
    r = _run(nc, [arrays], core_ids=[0])
    return r.results[0]["out_0"]
```

```python
from contextlib import ExitStack

import concourse.bass as bass
from concourse import mybir

F32 = mybir.dt.float32
F32R = mybir.dt.float32r
ALU = mybir.AluOpType
ACT = mybir.ActivationFunctionType
AX_X = mybir.AxisListType.X

P = 128
GROUPS = 32
EPS = (1e-5, 1e-6)
BANK = 512
VECTORS = ("gamma", "beta", "bq", "bk", "bv", "bp")


def two_attention_layers(nc, x, layers, vectors, out):
    IMAGES, N, C = x.shape
    LAYERS = len(layers)
    UNITS = IMAGES * LAYERS
    KC = C // P
    NB = N // P
    HALVES = N // BANK
    BPH = NB // HALVES
    PER_GROUP = C // GROUPS
    WX = C + 2
    SCALE = 1.0 / 16.0
    NV = len(VECTORS)
    TQ = KC * HALVES
    NR = NB // 2
    assert C == 256 and N == 1024 and IMAGES == 2 and LAYERS == 2

    x_rows = x.rearrange("b (p k) c -> b p k c", k=NB)
    bp_of_layers = vectors.rearrange("(l v) c -> v l c", v=NV)[VECTORS.index("bp"):VECTORS.index("bp") + 1, :, :]
    out_rows = out.rearrange("b (p k) c -> b p k c", k=NB)

    with ExitStack() as ctx:
        def sb(name, shape, dt=F32):
            return ctx.enter_context(nc.sbuf_tensor(name, shape, dt))

        def ps(name, shape):
            return ctx.enter_context(nc.psum_tensor(name, shape, F32))

        def sem(name):
            return ctx.enter_context(nc.semaphore(name))

        ident = sb("ident", [P, P])
        group_mean = sb("group_mean", [P, P])
        ones = sb("ones", [P, P])
        minus_half = sb("minus_half", [P, KC])
        xnat = sb("xnat", [P, IMAGES, NB, C])
        w_raw = {(l, k): sb(f"w_{k}{l}", [P, KC, C]) for l in range(LAYERS) for k in ("wq", "wk", "wv", "wp")}
        vec_rows = sb("vec_rows", [LAYERS * NV, C])
        vec_cols = sb("vec_cols", [P, KC, LAYERS * NV])
        bp_rows = sb("bp_rows", [1, LAYERS * C])
        bq_wide = sb("bq_wide", [P, LAYERS, KC, P])
        bv_wide = sb("bv_wide", [P, LAYERS, KC, P])
        wqT = sb("wqT", [P, LAYERS, KC, C])
        wkT_bk = sb("wkT_bk", [P, LAYERS, KC, C + 1])
        wvT = sb("wvT", [P, LAYERS, KC, C])
        A_hi = sb("A_hi", [P, LAYERS, KC, C], F32R)
        A_lo = sb("A_lo", [P, LAYERS, KC, C], F32R)
        Ac_hi = sb("Ac_hi", [P, KC, C], F32R)
        Ac_lo = sb("Ac_lo", [P, KC, C], F32R)
        Wx_hi = sb("Wx_hi", [P, LAYERS, KC, WX], F32R)
        Wx_lo = sb("Wx_lo", [P, LAYERS, KC, WX], F32R)
        G0, B0, E0, NNORM = 0, KC, 2 * KC, 2 * KC + 1
        U0, D0, NATT = 0, KC, KC + 1
        norm_all = sb("norm_all", [P, LAYERS, NNORM])
        att_all = sb("att_all", [P, LAYERS, NATT])
        norm = sb("norm", [P, NNORM])
        att = sb("att", [P, NATT])
        out_bias = sb("out_bias", [P, LAYERS, C])
        xstat = sb("xstat", [P, NB, C])
        xraw = sb("xraw", [P, KC, N])
        xn = sb("xn", [P, KC, N])
        xn_hi = sb("xn_hi", [P, KC, N], F32R)
        xn_lo = sb("xn_lo", [P, KC, N], F32R)
        t_hi = sb("t_hi", [P, KC, N + P], F32R)
        t_lo = sb("t_lo", [P, KC, N + P], F32R)
        tb_hi = sb("tb_hi", [P, 2, KC, P], F32R)
        tb_lo = sb("tb_lo", [P, 2, KC, P], F32R)
        V = sb("V", [P, NB, 2 * C], F32R)
        w_row = sb("w_row", [P, NB])
        probs = sb("probs", [P, 2, N])
        pT_hi = sb("pT_hi", [P, 2, NB, P], F32R)
        pT_lo = sb("pT_lo", [P, 2, NB, P], F32R)
        neg_max = sb("neg_max", [P, 2])
        exp_bias = sb("exp_bias", [P, 2])
        row_sum = sb("row_sum", [P, NB])
        row_inv = sb("row_inv", [P, 2])
        part_out = sb("part_out", [P, 2, C])
        bn = sb("bn", [P, KC, NR, 6])
        mv = sb("mv", [P, KC, 2])
        gmean = sb("gmean", [P, KC])
        dev = sb("dev", [P, KC])
        dev2 = sb("dev2", [P, KC])
        var_c = sb("var_c", [P, KC])
        var_e = sb("var_e", [P, KC])
        r0 = sb("r0", [P, KC])
        r0sq = sb("r0sq", [P, KC])
        r_err = sb("r_err", [P, KC])
        rstd = sb("rstd", [P, KC])
        gain = sb("gain", [P, KC])
        gain_mean = sb("gain_mean", [P, KC])
        shift = sb("shift", [P, KC])

        S = [ps(f"S{i}", [P, N]) for i in range(2)]
        T0 = ps("T0", [P, BANK])
        T1 = ps("T1", [P, BANK])
        O = ps("O", [P, BANK])
        X = ps("X", [P, BANK])
        PT = [T0, T1]
        T_RING = [T0, T1, O, X]
        V_RING = [T0, T1, O]

        ld_x = [[sem(f"ld_x{b}_{r}") for r in range(NR)] for b in range(IMAGES)]
        ld_w = {(l, k): sem(f"ld_{k}{l}") for l in range(LAYERS) for k in ("wq", "wk", "wv", "wp")}
        ld_vec = sem("ld_vec")
        stored = sem("stored")
        po_const = sem("po_const")
        po_block = sem("po_block")
        po_norm = sem("po_norm")
        po_resid = sem("po_resid")
        po_unit = sem("po_unit")
        po_r0 = sem("po_r0")
        pe_vec = sem("pe_vec")
        pe_wT = sem("pe_wT")
        pe_A = sem("pe_A")
        pe_Wx = sem("pe_Wx")
        pe_small = sem("pe_small")
        pe_ob = sem("pe_ob")
        pe_xT = sem("pe_xT")
        pe_gm = sem("pe_gm")
        pe_gv = sem("pe_gv")
        pe_t = sem("pe_t")
        pe_S = sem("pe_S")
        pe_V = sem("pe_V")
        pe_pT = sem("pe_pT")
        pe_O = sem("pe_O")
        ac_xstat = sem("ac_xstat")
        ac_wT = sem("ac_wT")
        ac_A = sem("ac_A")
        ac_Wx = sem("ac_Wx")
        ac_xT = sem("ac_xT")
        ac_t = sem("ac_t")
        ac_V = sem("ac_V")
        ac_P = sem("ac_P")
        ac_pT = sem("ac_pT")
        ac_xh = sem("ac_xh")
        dv_const = sem("dv_const")
        dv_vec = sem("dv_vec")
        dv_norm = sem("dv_norm")
        dv_wide = sem("dv_wide")
        dv_wT = sem("dv_wT")
        dv_A = sem("dv_A")
        dv_Wx = sem("dv_Wx")
        dv_small = sem("dv_small")
        dv_ob = sem("dv_ob")
        dv_bn = sem("dv_bn")
        dv_stat = sem("dv_stat")
        dv_t = sem("dv_t")
        dv_V = sem("dv_V")
        dv_max = sem("dv_max")
        dv_bias = sem("dv_bias")
        dv_pT = sem("dv_pT")
        dv_inv = sem("dv_inv")
        dv_part = sem("dv_part")
        dv_O = sem("dv_O")
        dv_xn = sem("dv_xn")
        dv_xl = sem("dv_xl")
        FIRST = 1
        AGGR, DEV, DEV2, VARC, VARE, R0SQ, RERR, RSTD, GAIN, GMUL, SHIFT = range(1, 12)
        STAT = SHIFT


        block = ctx.enter_context(nc.Block())

        @block.sync
        def _(sp):
            def load_image(b):
                for r in range(NR):
                    sp.dma_start(xnat[:, b, 2 * r:2 * r + 2, :], x_rows[b, :, 2 * r:2 * r + 2, :]).then_inc(ld_x[b][r], 16)

            load_image(0)
            for l in range(LAYERS):
                for name in ("wq", "wk", "wv", "wp"):
                    sp.dma_start(w_raw[l, name][:], layers[l][name].rearrange("(k p) d -> p k d", p=P)
                                 ).then_inc(ld_w[l, name], 16)
            for b in range(1, IMAGES):
                load_image(b)
            with sp.Fori(0, IMAGES) as b:
                for i in range(NB):
                    sp.wait_ge(dv_O, FIRST + b * NB + (UNITS - IMAGES) * NB + i + 1)
                    sp.dma_start(out_rows[bass.ds(b, 1), :, i:i + 1, :], xnat[:, bass.ds(b, 1), i:i + 1, :]
                                 ).then_inc(stored, 16)
            sp.wait_ge(stored, 16 * IMAGES * NB)

        @block.gpsimd
        def _(pool):
            nc.gpsimd.memset(ident[:], 1.0).then_inc(po_const, 1)
            nc.gpsimd.memset(group_mean[:], 1.0 / PER_GROUP).then_inc(po_const, 1)
            pool.wait_ge(po_const, 2)
            nc.gpsimd.affine_select(out=ident[:], in_=ident[:], compare_op=ALU.is_equal, fill=0.0, base=0,
                                    pattern=[[-1, P]], channel_multiplier=1).then_inc(po_const, 1)
            gv = group_mean[:, :].rearrange("p (g j) -> p g j", j=PER_GROUP)
            nc.gpsimd.affine_select(out=gv, in_=gv, compare_op=ALU.is_ge, fill=0.0, base=0,
                                    pattern=[[-PER_GROUP, P // PER_GROUP], [0, PER_GROUP]],
                                    channel_multiplier=1).then_inc(po_const, 1)
            pool.wait_ge(po_const, 4)
            nc.gpsimd.affine_select(out=gv, in_=gv, compare_op=ALU.is_ge, fill=0.0, base=PER_GROUP - 1,
                                    pattern=[[PER_GROUP, P // PER_GROUP], [0, PER_GROUP]],
                                    channel_multiplier=-1).then_inc(po_const, 1)

            def layer_of(tile, l):
                return tile[:, bass.ds(l, 1)].rearrange("p a k c -> p (a k) c")

            def norm_parameters(l):
                nc.gpsimd.tensor_copy(norm[:], norm_all[:, bass.ds(l, 1), :].rearrange("p a n -> p (a n)")).then_inc(po_norm, 1)

            def power(v):
                pool.wait_ge(dv_stat, v * STAT + VARE)
                nc.gpsimd.tensor_tensor(r0[:], var_e[:], minus_half[:], ALU.pow).then_inc(po_r0, 1)

            def unit_constants(l):
                nc.gpsimd.tensor_copy(att[:], att_all[:, bass.ds(l, 1), :].rearrange("p a n -> p (a n)"))
                nc.gpsimd.tensor_copy(Ac_hi[:], layer_of(A_hi, l)).then_inc(po_unit, 1)
                nc.gpsimd.tensor_copy(Ac_lo[:], layer_of(A_lo, l)).then_inc(po_unit, 1)

            pool.wait_ge(dv_norm, 1)
            norm_parameters(0)
            power(0)
            pool.wait_ge(ac_A, KC)
            nc.gpsimd.tensor_copy(A_hi[:, 0], Ac_hi[:])
            pool.wait_ge(dv_A, KC)
            nc.gpsimd.tensor_copy(A_lo[:, 0], Ac_lo[:]).then_inc(po_unit, 1)
            pool.wait_ge(dv_small, 1)
            nc.gpsimd.tensor_copy(att[:], att_all[:, 0, :]).then_inc(po_unit, 1)
            pool.wait_ge(pe_xT, NR)
            pool.wait_ge(dv_ob, LAYERS)
            pool.wait_ge(dv_A, LAYERS * KC)

            def t_block(u, i, parity):
                for src, dst in ((t_hi, tb_hi), (t_lo, tb_lo)):
                    nc.gpsimd.tensor_copy(dst[:, parity], src[:, :, bass.ds(i * P, P)]).then_inc(po_block, 1)

            def residual(u, i):
                rows = xnat[:, bass.ds(u % IMAGES, 1), bass.ds(i, 1), :].rearrange("p a b c -> p (a b) c")
                nc.gpsimd.tensor_tensor(rows, rows, out_bias[:, bass.ds(u // IMAGES, 1), :], ALU.add).then_inc(po_resid, 1)

            def unit(u, last):
                if not last:
                    norm_parameters((u + 1) // IMAGES)
                pool.wait_ge(dv_t, u * TQ + TQ)
                pool.wait_ge(dv_O, FIRST + u * NB)
                residual(u, 0)
                t_block(u, 2, 0)
                residual(u, 1)
                if not last:
                    power(u + 1)
                with pool.Fori(0, NB // 2 - 1) as j:
                    for k in range(2):
                        i = 2 * j + k
                        pool.wait_ge(pe_S, u * NB + i + 2)
                        t_block(u, i + 3, 1 - k)
                        residual(u, i + 2)
                if not last:
                    pool.wait_ge(dv_V, u * NB + NB)
                    unit_constants((u + 1) // IMAGES)

            with pool.Fori(0, UNITS - 1) as u:
                unit(u, False)
            unit(UNITS - 1, True)

        @block.scalar
        def _(act):
            act.dma_start(vec_rows[:], vectors).then_inc(ld_vec, 16)
            act.dma_start(bp_rows[0:1, :].rearrange("a (l c) -> a l c", l=LAYERS), bp_of_layers).then_inc(ld_vec, 16)

            def raw_rows(v, r, bank):
                act.wait_ge(pe_xT, v * NR + r + 1)
                nc.scalar.copy(xraw[:, :, 2 * r * P:2 * (r + 1) * P], bank.rearrange("p (k n) -> p k n", k=KC)
                               ).then_inc(ac_xT, 1)

            def weights(l):
                act.wait_ge(pe_wT, 3 * l + 1)
                nc.scalar.copy(wqT[:, l], T0[:, :].rearrange("p (k c) -> p k c", k=KC)).then_inc(ac_wT, 1)
                act.wait_ge(pe_wT, 3 * l + 3)
                nc.scalar.copy(wvT[:, l], O[:, :].rearrange("p (k c) -> p k c", k=KC)).then_inc(ac_wT, 1)
                for k in range(KC):
                    act.wait_ge(pe_A, KC * l + k + 1)
                    nc.scalar.activation((A_hi[:, l] if l else Ac_hi)[:, k, :], S[0][:, k * BANK:k * BANK + C], ACT.Identity, scale=SCALE)
                    nc.scalar.activation(Wx_hi[:, l, k, C:C + 1], S[0][:, k * BANK + C:k * BANK + C + 1],
                                         ACT.Identity, scale=SCALE).then_inc(ac_A, 1)
                for k in range(KC):
                    act.wait_ge(pe_Wx, KC * l + k + 1)
                    nc.scalar.copy(Wx_hi[:, l, k, 0:C], S[1][:, k * BANK:k * BANK + C]).then_inc(ac_Wx, 1)

            def xn_high(v):
                for q in range(TQ):
                    h, k = divmod(q, KC)
                    act.wait_ge(dv_xn, v * KC + k + 1)
                    cols = slice(h * BANK, (h + 1) * BANK)
                    nc.scalar.copy(xn_hi[:, k, cols], xn[:, k, cols]).then_inc(ac_xh, 1)

            for r in range(NR):
                raw_rows(0, r, S[r // 2][:, (r % 2) * BANK:(r % 2 + 1) * BANK])
            weights(0)
            xn_high(0)
            weights(1)
            for r in range(NR):
                act.wait_ge(ld_x[1][r], 16)

            def v_high(u, m):
                act.wait_ge(pe_V, u * NB + m + 1)
                nc.scalar.copy(V[:, m, 0:C], V_RING[m % 3][:, 0:C]).then_inc(ac_V, 1)

            def exponentials(u, i, parity):
                act.wait_ge(dv_bias, u * NB + i + 1)
                nc.scalar.activation(probs[:, parity, :], S[parity][:], ACT.Exp, bias=exp_bias[:, parity:parity + 1],
                                     accum_out=row_sum[:, bass.ds(i, 1)]).then_inc(ac_P, 1)

            def p_high(u, i, parity):
                for h in range(HALVES):
                    act.wait_ge(pe_pT, (u * NB + i) * HALVES + h + 1)
                    nc.scalar.copy(pT_hi[:, parity, h * BPH:(h + 1) * BPH, :],
                                   PT[h][:, :].rearrange("p (m n) -> p m n", m=BPH)).then_inc(ac_pT, 1)

            def unit(u, last):
                if not last:
                    act.wait_ge(dv_O, FIRST + u * NB)
                for q in range(TQ):
                    if not last:
                        nc.scalar.copy(xstat[:, 2 * q:2 * q + 2, :], xnat[:, bass.ds((u + 1) % IMAGES, 1), 2 * q:2 * q + 2, :]
                                       .rearrange("p a b c -> p (a b) c")).then_inc(ac_xstat, 1)
                    h, k = divmod(q, KC)
                    act.wait_ge(pe_t, u * TQ + q + 1)
                    nc.scalar.activation(t_hi[:, k, h * BANK:(h + 1) * BANK], T_RING[q][:], ACT.Identity,
                                         bias=att[:, U0 + k:U0 + k + 1]).then_inc(ac_t, 1)
                for m in range(NB):
                    v_high(u, m)
                    if m == 1:
                        exponentials(u, 0, 0)
                    if not last and m < NR:
                        raw_rows(u + 1, m, X[:])
                p_high(u, 0, 0)
                exponentials(u, 1, 1)
                with act.Fori(0, NB // 2 - 1) as j:
                    for k in range(2):
                        i = 2 * j + k
                        p_high(u, i + 1, 1 - k)
                        exponentials(u, i + 2, k)
                p_high(u, NB - 1, 1)
                if not last:
                    xn_high(u + 1)

            with act.Fori(0, UNITS - 1) as u:
                unit(u, False)
            unit(UNITS - 1, True)

        @block.vector
        def _(dve):
            nc.vector.memset(ones[:], 1.0).then_inc(dv_O, FIRST)
            nc.vector.memset(minus_half[:], -0.5)
            for t in (t_hi, t_lo):
                nc.vector.memset(t[:, :, N:].bitcast(F32), 0.0)
            for l in range(LAYERS):
                nc.vector.memset(norm_all[:, l, E0:E0 + 1], EPS[l])
                for wx in (Wx_hi, Wx_lo):
                    last = nc.vector.memset(wx[:, l, :, C + 1:WX].bitcast(F32), 0.0)
            last.then_inc(dv_const, 1)
            dve.wait_ge(dv_const, 1)

            def statistics_of(v, r):
                dve.wait_ge(ac_xT, v * NR + r + 1)
                for k in range(KC):
                    last = nc.vector.bn_stats(bn[:, k, r, :], xraw[:, k, 2 * r * P:2 * (r + 1) * P])
                last.then_inc(dv_bn, 1)

            def spread_vectors():
                dve.wait_ge(pe_vec, 1)
                nc.vector.tensor_copy(vec_cols[:], O[:, 0:KC * LAYERS * NV].rearrange("p (k r) -> p k r", k=KC)
                                      ).then_inc(dv_vec, 1)
                dve.wait_ge(dv_vec, 1)
                for l in range(LAYERS):
                    for n, at in (("gamma", G0), ("beta", B0)):
                        last = nc.vector.tensor_copy(norm_all[:, l, at:at + KC], vec_cols[:, :, l * NV + VECTORS.index(n)])
                last.then_inc(dv_norm, 1)

            def wide_vectors(l):
                nc.vector.tensor_copy(wkT_bk[:, l, :, C], vec_cols[:, :, l * NV + VECTORS.index("bk")])
                for n, wide in (("bq", bq_wide), ("bv", bv_wide)):
                    r = l * NV + VECTORS.index(n)
                    for k in range(KC):
                        last = nc.vector.tensor_scalar(wide[:, l, k, :], ones[:], vec_cols[:, k, r:r + 1], None, ALU.mult)
                last.then_inc(dv_wide, 1)

            def wk_transposed(l):
                dve.wait_ge(pe_wT, 3 * l + 2)
                nc.vector.tensor_copy(wkT_bk[:, l, :, 0:C], T1[:, :].rearrange("p (k c) -> p k c", k=KC)).then_inc(dv_wT, 1)

            def weights(l):
                hi, lo = (A_hi[:, l], A_lo[:, l]) if l else (Ac_hi, Ac_lo)
                for k in range(KC):
                    dve.wait_ge(ac_A, KC * l + k + 1)
                    nc.vector.scalar_tensor_tensor(lo[:, k, :], S[0][:, k * BANK:k * BANK + C], SCALE,
                                                   hi[:, k, :].bitcast(F32), ALU.mult, ALU.subtract)
                    nc.vector.scalar_tensor_tensor(Wx_lo[:, l, k, C:C + 1], S[0][:, k * BANK + C:k * BANK + C + 1], SCALE,
                                                   Wx_hi[:, l, k, C:C + 1].bitcast(F32), ALU.mult, ALU.subtract
                                                   ).then_inc(dv_A, 1)
                for k in range(KC):
                    dve.wait_ge(ac_Wx, KC * l + k + 1)
                    nc.vector.tensor_tensor(Wx_lo[:, l, k, 0:C], S[1][:, k * BANK:k * BANK + C],
                                            Wx_hi[:, l, k, 0:C].bitcast(F32), ALU.subtract).then_inc(dv_Wx, 1)
                dve.wait_ge(pe_small, l + 1)
                nc.vector.tensor_scalar(att_all[:, l, U0:U0 + KC], T1[:, 0:KC], SCALE, None, ALU.mult)
                nc.vector.tensor_scalar(att_all[:, l, D0:D0 + 1], T1[:, KC:KC + 1], SCALE, None, ALU.mult).then_inc(dv_small, 1)
                dve.wait_ge(pe_ob, l + 1)
                nc.vector.tensor_copy(out_bias[:, l, :], T0[:, 0:C]).then_inc(dv_ob, 1)

            def group_statistics(v):
                at = v * STAT
                for k in range(KC):
                    last = nc.vector.bn_aggr(mv[:, k, :], bn[:, k, :, :].rearrange("p b s -> p (b s)"))
                last.then_inc(dv_stat, 1)
                dve.wait_ge(pe_gm, v + 1)
                nc.vector.tensor_copy(gmean[:], X[:, 0:KC])
                dve.wait_ge(dv_stat, at + AGGR)
                nc.vector.tensor_tensor(dev[:], mv[:, :, 0], X[:, 0:KC], ALU.subtract).then_inc(dv_stat, 1)
                dve.wait_ge(dv_stat, at + DEV)
                nc.vector.tensor_tensor(dev2[:], dev[:], dev[:], ALU.mult).then_inc(dv_stat, 1)
                dve.wait_ge(dv_stat, at + DEV2)
                nc.vector.tensor_tensor(var_c[:], dev2[:], mv[:, :, 1], ALU.add).then_inc(dv_stat, 1)

            def variance(v):
                dve.wait_ge(pe_gv, v + 1)
                dve.wait_ge(po_norm, v + 1)
                nc.vector.tensor_scalar(var_e[:], X[:, 0:KC], norm[:, E0:E0 + 1], None, ALU.add).then_inc(dv_stat, 1)

            def affine_map(v):
                at = v * STAT
                dve.wait_ge(po_r0, v + 1)
                nc.vector.tensor_tensor(r0sq[:], r0[:], r0[:], ALU.mult).then_inc(dv_stat, 1)
                dve.wait_ge(dv_stat, at + R0SQ)
                nc.vector.scalar_tensor_tensor(r_err[:], r0sq[:], -0.5, var_e[:], ALU.mult, ALU.mult).then_inc(dv_stat, 1)
                dve.wait_ge(dv_stat, at + RERR)
                nc.vector.scalar_tensor_tensor(rstd[:], r_err[:], 1.5, r0[:], ALU.add, ALU.mult).then_inc(dv_stat, 1)
                dve.wait_ge(dv_stat, at + RSTD)
                nc.vector.tensor_tensor(gain[:], rstd[:], norm[:, G0:G0 + KC], ALU.mult).then_inc(dv_stat, 1)
                dve.wait_ge(dv_stat, at + GAIN)
                nc.vector.tensor_tensor(gain_mean[:], gain[:], gmean[:], ALU.mult).then_inc(dv_stat, 1)
                dve.wait_ge(dv_stat, at + GMUL)
                nc.vector.tensor_tensor(shift[:], norm[:, B0:B0 + KC], gain_mean[:], ALU.subtract).then_inc(dv_stat, 1)

            def normalise(v):
                dve.wait_ge(dv_stat, v * STAT + SHIFT)
                for k in range(KC):
                    nc.vector.tensor_scalar(xn[:, k, :], xraw[:, k, :], gain[:, k:k + 1], shift[:, k:k + 1],
                                            ALU.mult, ALU.add).then_inc(dv_xn, 1)

            def xn_low(v, h):
                for k in range(KC):
                    dve.wait_ge(ac_xh, v * TQ + h * KC + k + 1)
                    cols = slice(h * BANK, (h + 1) * BANK)
                    nc.vector.tensor_tensor(xn_lo[:, k, cols], xn[:, k, cols], xn_hi[:, k, cols].bitcast(F32),
                                            ALU.subtract).then_inc(dv_xl, 1)

            for r in range(NR):
                statistics_of(0, r)
            dve.wait_ge(dv_bn, NR)
            group_statistics(0)
            spread_vectors()
            variance(0)
            wide_vectors(0)
            wk_transposed(0)
            affine_map(0)
            normalise(0)
            weights(0)
            xn_low(0, 0)
            wide_vectors(1)
            wk_transposed(1)
            xn_low(0, 1)
            weights(1)

            def v_low(u, m):
                bank = V_RING[m % 3]
                dve.wait_ge(ac_V, u * NB + m + 1)
                nc.vector.tensor_tensor(V[:, m, C:2 * C], bank[:, 0:C], V[:, m, 0:C].bitcast(F32), ALU.subtract)
                nc.vector.tensor_scalar(w_row[:, m:m + 1], bank[:, C:C + 1], att[:, D0:D0 + 1], None, ALU.add
                                        ).then_inc(dv_V, 1)

            def row_max(u, i, parity):
                dve.wait_ge(pe_S, u * NB + i + 1)
                nc.vector.tensor_reduce(neg_max[:, parity:parity + 1], S[parity][:], AX_X, ALU.max, negate=True
                                        ).then_inc(dv_max, 1)

            def bias_of(u, i, parity, first=False):
                dve.wait_ge(dv_V, u * NB + (i + 1 if first else NB))
                dve.wait_ge(dv_max, u * NB + i + 1)
                w = w_row[:, bass.ds(i, 1)]
                nc.vector.scalar_tensor_tensor(exp_bias[:, parity:parity + 1], neg_max[:, parity:parity + 1], w, w,
                                               ALU.subtract, ALU.add).then_inc(dv_bias, 1)

            def p_low(u, i, parity):
                for h in range(HALVES):
                    dve.wait_ge(ac_pT, (u * NB + i) * HALVES + h + 1)
                    nc.vector.tensor_tensor(pT_lo[:, parity, h * BPH:(h + 1) * BPH, :],
                                            PT[h][:, :].rearrange("p (m n) -> p m n", m=BPH),
                                            pT_hi[:, parity, h * BPH:(h + 1) * BPH, :].bitcast(F32),
                                            ALU.subtract).then_inc(dv_pT, 1)

            def output(u, i, parity, bank):
                nc.vector.reciprocal(row_inv[:, parity:parity + 1], row_sum[:, bass.ds(i, 1)]).then_inc(dv_inv, 1)
                dve.wait_ge(dv_inv, u * NB + i + 1)
                dve.wait_ge(pe_O, u * NB + i + 1)
                dve.wait_ge(po_resid, u * NB + i + 1)
                rows = xnat[:, bass.ds(u % IMAGES, 1), bass.ds(i, 1), :].rearrange("p a b c -> p (a b c)")
                inv = row_inv[:, parity:parity + 1]
                nc.vector.scalar_tensor_tensor(part_out[:, parity, :], bank[:, C:2 * C], inv, rows,
                                               ALU.mult, ALU.add).then_inc(dv_part, 1)
                dve.wait_ge(dv_part, u * NB + i + 1)
                nc.vector.scalar_tensor_tensor(rows, bank[:, 0:C], inv, part_out[:, parity, :],
                                               ALU.mult, ALU.add).then_inc(dv_O, 1)

            def unit(u, last):
                for q in range(TQ):
                    h, k = divmod(q, KC)
                    dve.wait_ge(ac_t, u * TQ + q + 1)
                    cols = slice(h * BANK, (h + 1) * BANK)
                    nc.vector.scalar_tensor_tensor(t_lo[:, k, cols], T_RING[q][:], att[:, U0 + k:U0 + k + 1],
                                                   t_hi[:, k, cols].bitcast(F32), ALU.add, ALU.subtract
                                                   ).then_inc(dv_t, 1)
                row_max(u, 0, 0)
                for m in range(NB):
                    if not last and m == NR:
                        dve.wait_ge(dv_bn, (u + 1) * NR + NR)
                    v_low(u, m)
                    if m == 0:
                        bias_of(u, 0, 0, first=True)
                    if not last and m < NR:
                        statistics_of(u + 1, m)
                    if not last and m == NR:
                        group_statistics(u + 1)
                row_max(u, 1, 1)
                bias_of(u, 1, 1, first=True)
                if not last:
                    variance(u + 1)
                p_low(u, 0, 0)
                if not last:
                    affine_map(u + 1)
                    normalise(u + 1)
                with dve.Fori(0, NB // 2 - 1) as j:
                    for k in range(2):
                        i = 2 * j + k
                        row_max(u, i + 2, k)
                        bias_of(u, i + 2, k)
                        p_low(u, i + 1, 1 - k)
                        output(u, i, k, O)
                p_low(u, NB - 1, 1)
                if not last:
                    xn_low(u + 1, 0)
                output(u, NB - 2, 0, O)
                if not last:
                    xn_low(u + 1, 1)
                output(u, NB - 1, 1, X)

            with dve.Fori(0, UNITS - 1) as u:
                unit(u, False)
            unit(UNITS - 1, True)

        @block.tensor
        def _(pe):
            def passes(bank, pairs, start=True):
                todo = [(lo_s, hi_m) for (_, lo_s), (hi_m, _) in pairs]
                todo += [p for (hi_s, _), (hi_m, lo_m) in pairs for p in ((hi_s, lo_m), (hi_s, hi_m))]
                for n, (stationary, moving) in enumerate(todo):
                    last = nc.tensor.matmul(bank, stationary, moving, start=(n == 0), stop=(n == len(todo) - 1))
                return last

            def weights(l):
                for n, (name, bank) in enumerate((("wq", T0), ("wk", T1), ("wv", O))):
                    pe.wait_ge(ld_w[l, name], 16)
                    if l:
                        pe.wait_ge(*((dv_ob, 1), (dv_small, 1), (ac_wT, 2))[n])
                    for kd in range(KC):
                        for kc in range(KC):
                            last = nc.tensor.transpose(bank[:, kd * C + kc * P:kd * C + (kc + 1) * P],
                                                       w_raw[l, name][:, kc, kd * P:(kd + 1) * P], ident[:])
                    last.then_inc(pe_wT, 1)
                pe.wait_ge(ac_wT, 2 * l + 1)
                pe.wait_ge(dv_wT, l + 1)
                pe.wait_ge(dv_wide, l + 1)
                for mc in range(KC):
                    if l:
                        pe.wait_ge(dv_A, mc + 1)
                    for kd in range(KC):
                        last = nc.tensor.matmul(S[0][:, mc * BANK:mc * BANK + C + 1], wqT[:, l, kd, mc * P:(mc + 1) * P],
                                                wkT_bk[:, l, kd, :], start=(kd == 0), stop=(kd == KC - 1))
                    last.then_inc(pe_A, 1)
                pe.wait_ge(ac_wT, 2 * l + 2)
                pe.wait_ge(ld_w[l, "wp"], 16)
                for mc in range(KC):
                    if l:
                        pe.wait_ge(dv_Wx, mc + 1)
                    for kd in range(KC):
                        last = nc.tensor.matmul(S[1][:, mc * BANK:mc * BANK + C], wvT[:, l, kd, mc * P:(mc + 1) * P],
                                                w_raw[l, "wp"][:, kd, :], start=(kd == 0), stop=(kd == KC - 1))
                    last.then_inc(pe_Wx, 1)
                for mc in range(KC):
                    for kd in range(KC):
                        r = l * NV + VECTORS.index("bq")
                        nc.tensor.matmul(T1[:, mc:mc + 1], wkT_bk[:, l, kd, mc * P:(mc + 1) * P],
                                         vec_cols[:, kd, r:r + 1], start=(kd == 0), stop=(kd == KC - 1))
                for kd in range(KC):
                    r = l * NV + VECTORS.index("bk")
                    last = nc.tensor.matmul(T1[:, KC:KC + 1], bq_wide[:, l, kd, :], vec_cols[:, kd, r:r + 1],
                                            start=(kd == 0), stop=(kd == KC - 1))
                last.then_inc(pe_small, 1)
                nc.tensor.matmul(T0[:, 0:C], ones[0:1, :], bp_rows[0:1, l * C:(l + 1) * C], start=True, stop=False)
                for kd in range(KC):
                    last = nc.tensor.matmul(T0[:, 0:C], bv_wide[:, l, kd, :], w_raw[l, "wp"][:, kd, :],
                                            start=False, stop=(kd == KC - 1))
                last.then_inc(pe_ob, 1)

            def transpose_rows(bank, rows, r):
                for k in range(KC):
                    for i in range(2):
                        last = nc.tensor.transpose(bank[:, (2 * k + i) * P:(2 * k + i + 1) * P],
                                                   rows[:, 2 * r + i, k * P:(k + 1) * P], ident[:])
                last.then_inc(pe_xT, 1)

            def mean_of_groups(v):
                pe.wait_ge(ac_xT, v * NR + NR)
                pe.wait_ge(dv_stat, v * STAT + AGGR)
                nc.tensor.matmul(X[:, 0:KC], group_mean[:], mv[:, :, 0], start=True, stop=True).then_inc(pe_gm, 1)

            def variance_of_groups(v):
                pe.wait_ge(dv_stat, v * STAT + VARC)
                nc.tensor.matmul(X[:, 0:KC], group_mean[:], var_c[:], start=True, stop=True).then_inc(pe_gv, 1)

            pe.wait_ge(po_const, 5)
            for r in range(NR):
                pe.wait_ge(ld_x[0][r], 16)
                transpose_rows(S[r // 2][:, (r % 2) * BANK:(r % 2 + 1) * BANK], xnat[:, 0], r)
            mean_of_groups(0)
            pe.wait_ge(ld_vec, 32)
            for k in range(KC):
                last = nc.tensor.transpose(O[:, k * LAYERS * NV:(k + 1) * LAYERS * NV], vec_rows[:, k * P:(k + 1) * P],
                                           ident[0:LAYERS * NV, 0:LAYERS * NV])
            last.then_inc(pe_vec, 1)
            variance_of_groups(0)
            pe.wait_ge(dv_vec, 1)
            weights(0)
            weights(1)
            pe.wait_ge(dv_ob, LAYERS)
            pe.wait_ge(dv_Wx, LAYERS * KC)

            def t_product(u):
                pe.wait_ge(po_unit, u * 2 + 2)
                for q in range(TQ):
                    h, k = divmod(q, KC)
                    cols = slice(h * BANK, (h + 1) * BANK)
                    if k == 0:
                        pe.wait_ge(dv_xl, u * TQ + (h + 1) * KC)
                    if q == 2:
                        pe.wait_ge(dv_O, FIRST + u * NB)
                    passes(T_RING[q][:], [((Ac_hi[:, kc, k * P:(k + 1) * P], Ac_lo[:, kc, k * P:(k + 1) * P]),
                                           (xn_hi[:, kc, cols], xn_lo[:, kc, cols])) for kc in range(KC)]
                           ).then_inc(pe_t, 1)

            def scores(u, i, parity, first=False):
                if first:
                    pe.wait_ge(dv_t, u * TQ + KC)
                    t_block = [t[:, :, i * P:(i + 1) * P] for t in (t_hi, t_lo)]
                else:
                    pe.wait_ge(po_block, (u * (NB - 1) + i - 2) * 2 + 2)
                    pe.wait_ge(ac_P, u * NB + i - 1)
                    t_block = [tb[:, parity] for tb in (tb_hi, tb_lo)]
                todo = []
                for kc in range(KC):
                    todo.append((t_block[1][:, kc, :], xn_hi, kc))
                    todo.append((t_block[0][:, kc, :], xn_lo, kc))
                    todo.append((t_block[0][:, kc, :], xn_hi, kc))
                for n, (stationary, moving, kc) in enumerate(todo):
                    for h in range(HALVES):
                        last = nc.tensor.matmul(S[parity][:, h * BANK:(h + 1) * BANK], stationary,
                                                moving[:, kc, h * BANK:(h + 1) * BANK],
                                                start=(n == 0), stop=(n == len(todo) - 1))
                last.then_inc(pe_S, 1)

            def values(u, m):
                if m < 3:
                    pe.wait_ge(dv_t, u * TQ + m + 1)
                else:
                    pe.wait_ge(dv_V, u * NB + m - 2)
                rows = slice(m * P, (m + 1) * P)
                l = bass.ds(u // IMAGES, 1)
                passes(V_RING[m % 3][:, 0:WX], [((xn_hi[:, kc, rows], xn_lo[:, kc, rows]),
                                                 (Wx_hi[:, l, kc, :].rearrange("p a c -> p (a c)"),
                                                  Wx_lo[:, l, kc, :].rearrange("p a c -> p (a c)")))
                                                for kc in range(KC)]).then_inc(pe_V, 1)

            def next_rows(u, r):
                pe.wait_ge(ac_xstat, u * NR + r + 1)
                if r == 0:
                    pe.wait_ge(dv_t, u * TQ + TQ)
                else:
                    pe.wait_ge(ac_xT, (u + 1) * NR + r)
                transpose_rows(X, xstat, r)

            def transpose_probs(u, i, parity, first=False):
                pe.wait_ge(ac_P, u * NB + i + 1)
                if first:
                    pe.wait_ge(dv_V, u * NB + NB)
                else:
                    pe.wait_ge(dv_pT, (u * NB + i) * HALVES)
                for h in range(HALVES):
                    for m in range(BPH):
                        at = (h * BPH + m) * P
                        last = nc.tensor.transpose(PT[h][:, m * P:(m + 1) * P], probs[:, parity, at:at + P], ident[:])
                    last.then_inc(pe_pT, 1)

            def attend(u, i, parity, bank):
                pe.wait_ge(dv_pT, (u * NB + i) * HALVES + HALVES)
                for m in range(NB):
                    nc.tensor.matmul(bank[:], pT_hi[:, parity, m, :], V[:, m, :], start=(m == 0), stop=False)
                    last = nc.tensor.matmul(bank[:, C:2 * C], pT_lo[:, parity, m, :], V[:, m, 0:C],
                                            start=False, stop=(m == NB - 1))
                last.then_inc(pe_O, 1)

            def unit(u, last):
                t_product(u)
                scores(u, 0, 0, first=True)
                for m in range(NB):
                    values(u, m)
                    if not last and m < NR:
                        next_rows(u, m)
                    if m == NR:
                        scores(u, 1, 1, first=True)
                        if not last:
                            mean_of_groups(u + 1)
                    if not last and m == NB - 2:
                        variance_of_groups(u + 1)
                transpose_probs(u, 0, 0, first=True)
                with pe.Fori(0, NB // 2 - 1) as j:
                    for k in range(2):
                        i = 2 * j + k
                        scores(u, i + 2, k)
                        transpose_probs(u, i + 1, 1 - k)
                        pe.wait_ge(dv_O, FIRST + u * NB + i)
                        attend(u, i, k, O)
                transpose_probs(u, NB - 1, 1)
                pe.wait_ge(dv_O, FIRST + u * NB + NB - 2)
                attend(u, NB - 2, 0, O)
                if not last:
                    pe.wait_ge(dv_stat, (u + 1) * STAT + VARE)
                attend(u, NB - 1, 1, X)

            with pe.Fori(0, UNITS - 1) as u:
                unit(u, False)
            unit(UNITS - 1, True)


_L0 = {"gamma": "L0_conv_gamma", "beta": "L0_conv_beta", "wq": "L0_conv_wq", "bq": "L0_conv_bq", "wk": "L0_conv_wk",
       "bk": "L0_conv_bk", "wv": "L0_conv_wv", "bv": "L0_conv_bv", "wp": "L0_conv_wp", "bp": "L0_conv_bp"}
_L1 = {"gamma": "L1_conv_gn_gamma", "beta": "L1_conv_gn_beta", "wq": "L1_conv_wq", "bq": "L1_conv_bq",
       "wk": "L1_conv_wk", "bk": "L1_conv_bk", "wv": "L1_conv_wv", "bv": "L1_conv_bv", "wp": "L1_conv_wo",
       "bp": "L1_conv_bo"}


def kernel(**inputs):
    import numpy as _np
    import concourse.bacc as _bacc
    from concourse import mybir as _mybir
    from concourse.bass_utils import run_bass_kernel_spmd as _run

    nc = _bacc.Bacc("TRN2", target_bir_lowering=False, num_devices=1)
    arrays = {}

    def dram(name, a):
        a = _np.ascontiguousarray(a)
        arrays[f"in_{name}"] = a
        return nc.dram_tensor(f"in_{name}", a.shape, _mybir.dt.from_np(a.dtype), kind="ExternalInput").ap()

    x = dram("x", inputs["x"])
    layers = [{k: dram(names[k], inputs[names[k]]) for k in ("wq", "wk", "wv", "wp")} for names in (_L0, _L1)]
    vectors = dram("vectors", _np.stack([inputs[names[k]] for names in (_L0, _L1) for k in VECTORS]))
    out = nc.dram_tensor("out_0", inputs["x"].shape, _mybir.dt.float32, kind="ExternalOutput").ap()
    two_attention_layers(nc, x.rearrange("b h w c -> b (h w) c"), layers, vectors,
                         out.rearrange("b h w c -> b (h w) c"))
    r = _run(nc, [arrays], core_ids=[0])
    return r.results[0]["out_0"]
```

```python
from contextlib import ExitStack

import concourse.bass as bass
from concourse import mybir

F32 = mybir.dt.float32
F32R = mybir.dt.float32r
ALU = mybir.AluOpType
ACT = mybir.ActivationFunctionType
AX_X = mybir.AxisListType.X

P = 128
GROUPS = 32
EPS = (1e-5, 1e-6)
BANK = 512
VECTORS = ("gamma", "beta", "bv", "bq", "bk", "bp")
WIDE = VECTORS[3:]


def two_attention_layers(nc, x, layers, vectors, out):
    IMAGES, N, C = x.shape
    LAYERS = len(layers)
    UNITS = IMAGES * LAYERS
    KC = C // P
    NB = N // P
    HALVES = N // BANK
    BPH = NB // HALVES
    PER_GROUP = C // GROUPS
    WX = C + 2
    SCALE = C ** -0.5
    NV = len(VECTORS)
    TQ = KC * HALVES
    NR = NB // 2
    assert C == 256 and N == 1024 and IMAGES == 2 and LAYERS == 2

    x_rows = x.rearrange("b (p k) c -> b p k c", k=NB)
    vectors_of_layer = vectors.rearrange("(a l v) c -> a l v c", a=1, v=NV)
    out_rows = out.rearrange("b (p k) c -> b p k c", k=NB)

    with ExitStack() as ctx:
        def sb(name, shape, dt=F32):
            return ctx.enter_context(nc.sbuf_tensor(name, shape, dt))

        def ps(name, shape):
            return ctx.enter_context(nc.psum_tensor(name, shape, F32))

        def sem(name):
            return ctx.enter_context(nc.semaphore(name))

        ident = sb("ident", [P, P])
        group_mean = sb("group_mean", [P, P])
        minus_half = sb("minus_half", [P, KC])
        xnat = sb("xnat", [P, IMAGES, NB, C])
        w_raw = {(l, k): sb(f"w_{k}{l}", [P, KC, C]) for l in range(LAYERS) for k in ("wq", "wk", "wv", "wp")}
        vec_rows = sb("vec_rows", [LAYERS * NV, C])
        vec_cols = sb("vec_cols", [P, KC, LAYERS * NV])
        wide = sb("wide", [P, LAYERS, len(WIDE), C])
        wqT = sb("wqT", [P, LAYERS, KC, C])
        wkT_bk = sb("wkT_bk", [P, LAYERS, KC, C + 1])
        wvT = sb("wvT", [P, LAYERS, KC, C])
        A_hi = sb("A_hi", [P, LAYERS, KC, C], F32R)
        A_lo = sb("A_lo", [P, LAYERS, KC, C], F32R)
        Ac_hi = sb("Ac_hi", [P, KC, C], F32R)
        Ac_lo = sb("Ac_lo", [P, KC, C], F32R)
        Wx_hi = sb("Wx_hi", [P, LAYERS, KC, WX], F32R)
        Wx_lo = sb("Wx_lo", [P, LAYERS, KC, WX], F32R)
        U0, D0, NATT = 0, KC, KC + 1
        att_all = sb("att_all", [P, LAYERS, NATT])
        products = sb("products", [P, LAYERS, NATT, C])
        att = sb("att", [P, NATT])
        eps_all = sb("eps_all", [P, LAYERS])
        eps = sb("eps", [P, 1])
        gamma_beta = sb("gamma_beta", [P, KC, 2])
        out_bias = sb("out_bias", [P, LAYERS, C])
        xstat = sb("xstat", [P, NB, C])
        xraw = sb("xraw", [P, KC, N])
        xn = sb("xn", [P, KC, N])
        xn_hi = sb("xn_hi", [P, KC, N], F32R)
        xn_lo = sb("xn_lo", [P, KC, N], F32R)
        t_hi = sb("t_hi", [P, KC, N + P], F32R)
        t_lo = sb("t_lo", [P, KC, N + P], F32R)
        tb_hi = sb("tb_hi", [P, 2, KC, P], F32R)
        tb_lo = sb("tb_lo", [P, 2, KC, P], F32R)
        V = sb("V", [P, NB, 2 * C], F32R)
        w_row = sb("w_row", [P, NB])
        probs = sb("probs", [P, 2, N])
        pT_hi = sb("pT_hi", [P, 2, NB, P], F32R)
        pT_lo = sb("pT_lo", [P, 2, NB, P], F32R)
        neg_max = sb("neg_max", [P, 2])
        exp_bias = sb("exp_bias", [P, 2])
        row_sum = sb("row_sum", [P, NB])
        row_inv = sb("row_inv", [P, 2])
        part_out = sb("part_out", [P, 2, C])
        bn = sb("bn", [P, KC, NR, 6])
        mv = sb("mv", [P, KC, 2])
        gmean = sb("gmean", [P, KC])
        dev = sb("dev", [P, KC])
        dev2 = sb("dev2", [P, KC])
        var_c = sb("var_c", [P, KC])
        var_e = sb("var_e", [P, KC])
        r0 = sb("r0", [P, KC])
        r0sq = sb("r0sq", [P, KC])
        r_err = sb("r_err", [P, KC])
        rstd = sb("rstd", [P, KC])
        gain = sb("gain", [P, KC])
        gain_mean = sb("gain_mean", [P, KC])
        shift = sb("shift", [P, KC])

        S = [ps(f"S{i}", [P, N]) for i in range(2)]
        T0 = ps("T0", [P, BANK])
        T1 = ps("T1", [P, BANK])
        O = ps("O", [P, BANK])
        X = ps("X", [P, BANK])
        PT = [T0, T1]
        T_RING = [T0, T1, O, X]
        V_RING = [T0, T1, O]

        ld_x = [[sem(f"ld_x{b}_{r}") for r in range(NR)] for b in range(IMAGES)]
        ld_w = {(l, k): sem(f"ld_{k}{l}") for l in range(LAYERS) for k in ("wq", "wk", "wv", "wp")}
        ld_vec = sem("ld_vec")
        ld_wide = [sem(f"ld_wide{l}") for l in range(LAYERS)]
        stored = sem("stored")
        po_const = sem("po_const")
        po_block = sem("po_block")
        po_bk = sem("po_bk")
        po_norm = sem("po_norm")
        po_resid = sem("po_resid")
        po_unit = sem("po_unit")
        po_r0 = sem("po_r0")
        pe_vec = sem("pe_vec")
        pe_wT = sem("pe_wT")
        pe_A = sem("pe_A")
        pe_Wx = sem("pe_Wx")
        pe_ob = sem("pe_ob")
        pe_xT = sem("pe_xT")
        pe_gm = sem("pe_gm")
        pe_gv = sem("pe_gv")
        pe_t = sem("pe_t")
        pe_S = sem("pe_S")
        pe_V = sem("pe_V")
        pe_pT = sem("pe_pT")
        pe_O = sem("pe_O")
        ac_xstat = sem("ac_xstat")
        ac_wT = sem("ac_wT")
        ac_A = sem("ac_A")
        ac_Wx = sem("ac_Wx")
        ac_xT = sem("ac_xT")
        ac_t = sem("ac_t")
        ac_V = sem("ac_V")
        ac_P = sem("ac_P")
        ac_pT = sem("ac_pT")
        ac_xh = sem("ac_xh")
        dv_const = sem("dv_const")
        dv_vec = sem("dv_vec")
        dv_A = sem("dv_A")
        dv_Wx = sem("dv_Wx")
        dv_ob = sem("dv_ob")
        dv_att = sem("dv_att")
        dv_bn = sem("dv_bn")
        dv_stat = sem("dv_stat")
        dv_xn = sem("dv_xn")
        dv_xl = sem("dv_xl")
        dv_t = sem("dv_t")
        dv_V = sem("dv_V")
        dv_max = sem("dv_max")
        dv_bias = sem("dv_bias")
        dv_pT = sem("dv_pT")
        dv_inv = sem("dv_inv")
        dv_part = sem("dv_part")
        dv_O = sem("dv_O")
        FIRST = 1
        AGGR, DEV, DEV2, VARC, VARE, R0SQ, RERR, RSTD, GAIN, GMUL, SHIFT = range(1, 12)
        STAT = SHIFT

        block = ctx.enter_context(nc.Block())

        @block.sync
        def _(sp):
            def load_image(b):
                for r in range(NR):
                    sp.dma_start(xnat[:, b, 2 * r:2 * r + 2, :], x_rows[b, :, 2 * r:2 * r + 2, :]
                                 ).then_inc(ld_x[b][r], 16)

            def load_weights(l, names):
                for name in names:
                    sp.dma_start(w_raw[l, name][:], layers[l][name].rearrange("(k p) d -> p k d", p=P)
                                 ).then_inc(ld_w[l, name], 16)

            def load_wide(l):
                at = VECTORS.index(WIDE[0])
                sp.dma_start(wide[:, l], vectors_of_layer[:, l, at:at + len(WIDE), :].to_broadcast([P, len(WIDE), C])
                             ).then_inc(ld_wide[l], 16)

            load_weights(0, ("wq", "wk"))
            load_image(0)
            load_weights(0, ("wv", "wp"))
            load_weights(1, ("wq", "wk"))
            load_wide(0)
            load_weights(1, ("wv", "wp"))
            load_wide(1)
            for b in range(1, IMAGES):
                load_image(b)
            with sp.Fori(0, IMAGES) as b:
                for i in range(NB):
                    sp.wait_ge(dv_O, FIRST + b * NB + (UNITS - IMAGES) * NB + i + 1)
                    sp.dma_start(out_rows[bass.ds(b, 1), :, i:i + 1, :], xnat[:, bass.ds(b, 1), i:i + 1, :]
                                 ).then_inc(stored, 16)
            sp.wait_ge(stored, 16 * IMAGES * NB)

        @block.gpsimd
        def _(pool):
            nc.gpsimd.memset(ident[:], 1.0).then_inc(po_const, 1)
            nc.gpsimd.memset(group_mean[:], 1.0 / PER_GROUP).then_inc(po_const, 1)
            pool.wait_ge(po_const, 2)
            nc.gpsimd.affine_select(out=ident[:], in_=ident[:], compare_op=ALU.is_equal, fill=0.0, base=0,
                                    pattern=[[-1, P]], channel_multiplier=1).then_inc(po_const, 1)
            gv = group_mean[:, :].rearrange("p (g j) -> p g j", j=PER_GROUP)
            nc.gpsimd.affine_select(out=gv, in_=gv, compare_op=ALU.is_ge, fill=0.0, base=0,
                                    pattern=[[-PER_GROUP, P // PER_GROUP], [0, PER_GROUP]],
                                    channel_multiplier=1).then_inc(po_const, 1)
            pool.wait_ge(po_const, 4)
            nc.gpsimd.affine_select(out=gv, in_=gv, compare_op=ALU.is_ge, fill=0.0, base=PER_GROUP - 1,
                                    pattern=[[PER_GROUP, P // PER_GROUP], [0, PER_GROUP]],
                                    channel_multiplier=-1).then_inc(po_const, 1)

            def layer_of(tile, l):
                return tile[:, bass.ds(l, 1)].rearrange("p a k c -> p (a k) c")

            def norm_parameters(l):
                nc.gpsimd.tensor_copy(eps[:], eps_all[:, bass.ds(l, 1)])
                nc.gpsimd.tensor_copy(gamma_beta[:], vec_cols[:, :, bass.ds(l * NV, 2)]).then_inc(po_norm, 1)

            def power(v):
                pool.wait_ge(dv_stat, v * STAT + VARE)
                nc.gpsimd.tensor_tensor(r0[:], var_e[:], minus_half[:], ALU.pow).then_inc(po_r0, 1)

            def unit_constants(l):
                nc.gpsimd.tensor_copy(att[:], att_all[:, bass.ds(l, 1), :].rearrange("p a n -> p (a n)"))
                nc.gpsimd.tensor_copy(Ac_hi[:], layer_of(A_hi, l)).then_inc(po_unit, 1)
                nc.gpsimd.tensor_copy(Ac_lo[:], layer_of(A_lo, l)).then_inc(po_unit, 1)

            pool.wait_ge(dv_const, 1)
            pool.wait_ge(dv_vec, 1)
            for l in range(LAYERS):
                nc.gpsimd.tensor_copy(wkT_bk[:, l, :, C], vec_cols[:, :, l * NV + VECTORS.index("bk")]
                                      ).then_inc(po_bk, 1)
            norm_parameters(0)
            power(0)
            pool.wait_ge(ac_A, KC)
            nc.gpsimd.tensor_copy(A_hi[:, 0], Ac_hi[:])
            pool.wait_ge(dv_A, KC)
            nc.gpsimd.tensor_copy(A_lo[:, 0], Ac_lo[:]).then_inc(po_unit, 1)
            pool.wait_ge(dv_att, NATT)
            nc.gpsimd.tensor_copy(att[:], att_all[:, 0, :]).then_inc(po_unit, 1)
            pool.wait_ge(pe_xT, NR)
            pool.wait_ge(dv_ob, LAYERS)
            pool.wait_ge(dv_att, LAYERS * NATT)
            pool.wait_ge(dv_A, LAYERS * KC)

            def t_block(u, i, parity):
                for src, dst in ((t_hi, tb_hi), (t_lo, tb_lo)):
                    nc.gpsimd.tensor_copy(dst[:, parity], src[:, :, bass.ds(i * P, P)]).then_inc(po_block, 1)

            def residual(u, i):
                rows = xnat[:, bass.ds(u % IMAGES, 1), bass.ds(i, 1), :].rearrange("p a b c -> p (a b) c")
                nc.gpsimd.tensor_tensor(rows, rows, out_bias[:, bass.ds(u // IMAGES, 1), :], ALU.add
                                        ).then_inc(po_resid, 1)

            def unit(u, last):
                if not last:
                    norm_parameters((u + 1) // IMAGES)
                pool.wait_ge(dv_t, u * TQ + TQ)
                pool.wait_ge(dv_O, FIRST + u * NB)
                residual(u, 0)
                t_block(u, 2, 0)
                residual(u, 1)
                if not last:
                    power(u + 1)
                with pool.Fori(0, NB // 2 - 1) as j:
                    for k in range(2):
                        i = 2 * j + k
                        pool.wait_ge(pe_S, u * NB + i + 2)
                        t_block(u, i + 3, 1 - k)
                        residual(u, i + 2)
                if not last:
                    pool.wait_ge(dv_V, u * NB + NB)
                    unit_constants((u + 1) // IMAGES)

            with pool.Fori(0, UNITS - 1) as u:
                unit(u, False)
            unit(UNITS - 1, True)

        @block.scalar
        def _(act):
            act.dma_start(vec_rows[:], vectors).then_inc(ld_vec, 16)

            def raw_rows(v, r, bank):
                act.wait_ge(pe_xT, v * NR + r + 1)
                nc.scalar.copy(xraw[:, :, 2 * r * P:2 * (r + 1) * P], bank.rearrange("p (k n) -> p k n", k=KC)
                               ).then_inc(ac_xT, 1)

            def weight_transposed(l, n):
                bank, dst = ((T0, wqT[:, l]), (T1, wkT_bk[:, l, :, 0:C]), (O, wvT[:, l]))[n]
                act.wait_ge(pe_wT, 3 * l + n + 1)
                nc.scalar.copy(dst, bank[:, :].rearrange("p (k c) -> p k c", k=KC)).then_inc(ac_wT, 1)

            def A_high(l, k):
                act.wait_ge(pe_A, KC * l + k + 1)
                nc.scalar.activation((A_hi[:, l] if l else Ac_hi)[:, k, :], S[0][:, k * BANK:k * BANK + C],
                                     ACT.Identity, scale=SCALE)
                nc.scalar.activation(Wx_hi[:, l, k, C:C + 1], S[0][:, k * BANK + C:k * BANK + C + 1],
                                     ACT.Identity, scale=SCALE).then_inc(ac_A, 1)

            def Wx_high(l):
                for k in range(KC):
                    act.wait_ge(pe_Wx, KC * l + k + 1)
                    nc.scalar.copy(Wx_hi[:, l, k, 0:C], S[1][:, k * BANK:k * BANK + C]).then_inc(ac_Wx, 1)

            def xn_high(v):
                for q in range(TQ):
                    h, k = divmod(q, KC)
                    act.wait_ge(dv_xn, v * TQ + q + 1)
                    cols = slice(h * BANK, (h + 1) * BANK)
                    nc.scalar.copy(xn_hi[:, k, cols], xn[:, k, cols]).then_inc(ac_xh, 1)

            weight_transposed(0, 0)
            weight_transposed(0, 1)
            for r in range(NR):
                raw_rows(0, r, S[1][:, (r % 2) * BANK:(r % 2 + 1) * BANK])
                if r == 2:
                    A_high(0, 0)
            A_high(0, 1)
            weight_transposed(0, 2)
            weight_transposed(1, 0)
            weight_transposed(1, 1)
            Wx_high(0)
            weight_transposed(1, 2)
            xn_high(0)
            A_high(1, 0)
            A_high(1, 1)
            Wx_high(1)
            for r in range(NR):
                act.wait_ge(ld_x[1][r], 16)

            def v_high(u, m):
                act.wait_ge(pe_V, u * NB + m + 1)
                nc.scalar.copy(V[:, m, 0:C], V_RING[m % 3][:, 0:C]).then_inc(ac_V, 1)

            def exponentials(u, i, parity):
                act.wait_ge(dv_bias, u * NB + i + 1)
                nc.scalar.activation(probs[:, parity, :], S[parity][:], ACT.Exp, bias=exp_bias[:, parity:parity + 1],
                                     accum_out=row_sum[:, bass.ds(i, 1)]).then_inc(ac_P, 1)

            def p_high(u, i, parity):
                for h in range(HALVES):
                    act.wait_ge(pe_pT, (u * NB + i) * HALVES + h + 1)
                    nc.scalar.copy(pT_hi[:, parity, h * BPH:(h + 1) * BPH, :],
                                   PT[h][:, :].rearrange("p (m n) -> p m n", m=BPH)).then_inc(ac_pT, 1)

            def unit(u, last):
                if not last:
                    act.wait_ge(dv_O, FIRST + u * NB)
                for q in range(TQ):
                    if not last:
                        rows = xnat[:, bass.ds((u + 1) % IMAGES, 1), 2 * q:2 * q + 2, :]
                        nc.scalar.copy(xstat[:, 2 * q:2 * q + 2, :], rows.rearrange("p a b c -> p (a b) c")
                                       ).then_inc(ac_xstat, 1)
                    h, k = divmod(q, KC)
                    act.wait_ge(pe_t, u * TQ + q + 1)
                    nc.scalar.activation(t_hi[:, k, h * BANK:(h + 1) * BANK], T_RING[q][:], ACT.Identity,
                                         bias=att[:, U0 + k:U0 + k + 1]).then_inc(ac_t, 1)
                for m in range(NB):
                    v_high(u, m)
                    if not last and m % 2 == 0:
                        raw_rows(u + 1, m // 2, X[:])
                    if m == 4:
                        exponentials(u, 0, 0)
                p_high(u, 0, 0)
                exponentials(u, 1, 1)
                with act.Fori(0, NB // 2 - 1) as j:
                    for k in range(2):
                        i = 2 * j + k
                        p_high(u, i + 1, 1 - k)
                        exponentials(u, i + 2, k)
                p_high(u, NB - 1, 1)
                if not last:
                    xn_high(u + 1)

            with act.Fori(0, UNITS - 1) as u:
                unit(u, False)
            unit(UNITS - 1, True)

        @block.vector
        def _(dve):
            nc.vector.memset(minus_half[:], -0.5)
            for t in (t_hi, t_lo):
                nc.vector.memset(t[:, :, N:].bitcast(F32), 0.0)
            for l in range(LAYERS):
                nc.vector.memset(eps_all[:, l:l + 1], EPS[l])
                for wx in (Wx_hi, Wx_lo):
                    last = nc.vector.memset(wx[:, l, :, C + 1:WX].bitcast(F32), 0.0)
            last.then_inc(dv_const, 1)
            dve.wait_ge(dv_const, 1)

            def statistics_of(v, r):
                dve.wait_ge(ac_xT, v * NR + r + 1)
                for k in range(KC):
                    last = nc.vector.bn_stats(bn[:, k, r, :], xraw[:, k, 2 * r * P:2 * (r + 1) * P])
                last.then_inc(dv_bn, 1)

            def A_low(l, k):
                hi, lo = (A_hi[:, l], A_lo[:, l]) if l else (Ac_hi, Ac_lo)
                dve.wait_ge(ac_A, KC * l + k + 1)
                nc.vector.scalar_tensor_tensor(lo[:, k, :], S[0][:, k * BANK:k * BANK + C], SCALE,
                                               hi[:, k, :].bitcast(F32), ALU.mult, ALU.subtract)
                nc.vector.scalar_tensor_tensor(Wx_lo[:, l, k, C:C + 1], S[0][:, k * BANK + C:k * BANK + C + 1], SCALE,
                                               Wx_hi[:, l, k, C:C + 1].bitcast(F32), ALU.mult, ALU.subtract
                                               ).then_inc(dv_A, 1)

            def Wx_low(l, k):
                dve.wait_ge(ac_Wx, KC * l + k + 1)
                nc.vector.tensor_tensor(Wx_lo[:, l, k, 0:C], S[1][:, k * BANK:k * BANK + C],
                                        Wx_hi[:, l, k, 0:C].bitcast(F32), ALU.subtract).then_inc(dv_Wx, 1)

            def attention_vector(l, n):
                bq, bk = (wide[:, l, WIDE.index(name), :] for name in ("bq", "bk"))
                dve.wait_ge(ld_wide[l], 16)
                nc.vector.tensor_tensor_reduce(out=products[:, l, n, :], in0=w_raw[l, "wk"][:, n, :] if n < KC else bk,
                                               in1=bq, scale=SCALE, scalar=0.0, op0=ALU.mult, op1=ALU.add,
                                               accum_out=att_all[:, l, n:n + 1]).then_inc(dv_att, 1)

            def output_bias(l, bank):
                dve.wait_ge(ld_wide[l], 16)
                dve.wait_ge(pe_ob, l + 1)
                nc.vector.tensor_tensor(out_bias[:, l, :], bank[:, 0:C], wide[:, l, WIDE.index("bp"), :], ALU.add
                                        ).then_inc(dv_ob, 1)

            def channel_statistics(v):
                for k in range(KC):
                    last = nc.vector.bn_aggr(mv[:, k, :], bn[:, k, :, :].rearrange("p b s -> p (b s)"))
                last.then_inc(dv_stat, 1)

            def group_deviation(v):
                at = v * STAT
                dve.wait_ge(pe_gm, v + 1)
                nc.vector.tensor_copy(gmean[:], X[:, 0:KC])
                dve.wait_ge(dv_stat, at + AGGR)
                nc.vector.tensor_tensor(dev[:], mv[:, :, 0], X[:, 0:KC], ALU.subtract).then_inc(dv_stat, 1)
                dve.wait_ge(dv_stat, at + DEV)
                nc.vector.tensor_tensor(dev2[:], dev[:], dev[:], ALU.mult).then_inc(dv_stat, 1)
                dve.wait_ge(dv_stat, at + DEV2)
                nc.vector.tensor_tensor(var_c[:], dev2[:], mv[:, :, 1], ALU.add).then_inc(dv_stat, 1)

            def variance(v):
                dve.wait_ge(pe_gv, v + 1)
                dve.wait_ge(po_norm, v + 1)
                nc.vector.tensor_scalar(var_e[:], X[:, 0:KC], eps[:], None, ALU.add).then_inc(dv_stat, 1)

            def affine_map(v):
                at = v * STAT
                dve.wait_ge(po_r0, v + 1)
                nc.vector.tensor_tensor(r0sq[:], r0[:], r0[:], ALU.mult).then_inc(dv_stat, 1)
                dve.wait_ge(dv_stat, at + R0SQ)
                nc.vector.scalar_tensor_tensor(r_err[:], r0sq[:], -0.5, var_e[:], ALU.mult, ALU.mult
                                               ).then_inc(dv_stat, 1)
                dve.wait_ge(dv_stat, at + RERR)
                nc.vector.scalar_tensor_tensor(rstd[:], r_err[:], 1.5, r0[:], ALU.add, ALU.mult).then_inc(dv_stat, 1)
                dve.wait_ge(dv_stat, at + RSTD)
                nc.vector.tensor_tensor(gain[:], rstd[:], gamma_beta[:, :, 0], ALU.mult).then_inc(dv_stat, 1)
                dve.wait_ge(dv_stat, at + GAIN)
                nc.vector.tensor_tensor(gain_mean[:], gain[:], gmean[:], ALU.mult).then_inc(dv_stat, 1)
                dve.wait_ge(dv_stat, at + GMUL)
                nc.vector.tensor_tensor(shift[:], gamma_beta[:, :, 1], gain_mean[:], ALU.subtract).then_inc(dv_stat, 1)

            def normalise(v):
                dve.wait_ge(dv_stat, v * STAT + SHIFT)
                for q in range(TQ):
                    h, k = divmod(q, KC)
                    cols = slice(h * BANK, (h + 1) * BANK)
                    nc.vector.tensor_scalar(xn[:, k, cols], xraw[:, k, cols], gain[:, k:k + 1], shift[:, k:k + 1],
                                            ALU.mult, ALU.add).then_inc(dv_xn, 1)

            def xn_low(v, h):
                for k in range(KC):
                    dve.wait_ge(ac_xh, v * TQ + h * KC + k + 1)
                    cols = slice(h * BANK, (h + 1) * BANK)
                    nc.vector.tensor_tensor(xn_lo[:, k, cols], xn[:, k, cols], xn_hi[:, k, cols].bitcast(F32),
                                            ALU.subtract).then_inc(dv_xl, 1)

            dve.wait_ge(pe_vec, 1)
            nc.vector.tensor_copy(vec_cols[:], O[:, 0:KC * LAYERS * NV].rearrange("p (k r) -> p k r", k=KC)
                                  ).then_inc(dv_vec, 1)
            statistics_of(0, 0)
            statistics_of(0, 1)
            statistics_of(0, 2)
            A_low(0, 0)
            statistics_of(0, 3)
            dve.wait_ge(dv_bn, NR)
            channel_statistics(0)
            A_low(0, 1)
            attention_vector(0, 0)
            group_deviation(0)
            attention_vector(0, 1)
            variance(0)
            Wx_low(0, 0)
            attention_vector(0, 2)
            affine_map(0)
            normalise(0)
            Wx_low(0, 1)
            output_bias(0, X)
            xn_low(0, 0)
            xn_low(0, 1)
            output_bias(1, O)
            dve.wait_ge(dv_ob, LAYERS)
            nc.vector.memset(w_row[:], 0.0).then_inc(dv_O, FIRST)
            for n in range(NATT):
                attention_vector(1, n)
            for k in range(KC):
                A_low(1, k)
            for k in range(KC):
                Wx_low(1, k)

            def v_low(u, m):
                bank = V_RING[m % 3]
                dve.wait_ge(ac_V, u * NB + m + 1)
                nc.vector.tensor_tensor(V[:, m, C:2 * C], bank[:, 0:C], V[:, m, 0:C].bitcast(F32), ALU.subtract)
                nc.vector.tensor_scalar(w_row[:, m:m + 1], bank[:, C:C + 1], att[:, D0:D0 + 1], None, ALU.add
                                        ).then_inc(dv_V, 1)

            def row_max(u, i, parity):
                dve.wait_ge(pe_S, u * NB + i + 1)
                nc.vector.tensor_reduce(neg_max[:, parity:parity + 1], S[parity][:], AX_X, ALU.max, negate=True
                                        ).then_inc(dv_max, 1)

            def bias_of(u, i, parity, first=False):
                dve.wait_ge(dv_V, u * NB + (i + 1 if first else NB))
                dve.wait_ge(dv_max, u * NB + i + 1)
                w = w_row[:, bass.ds(i, 1)]
                nc.vector.scalar_tensor_tensor(exp_bias[:, parity:parity + 1], neg_max[:, parity:parity + 1], w, w,
                                               ALU.subtract, ALU.add).then_inc(dv_bias, 1)

            def p_low(u, i, parity):
                for h in range(HALVES):
                    dve.wait_ge(ac_pT, (u * NB + i) * HALVES + h + 1)
                    nc.vector.tensor_tensor(pT_lo[:, parity, h * BPH:(h + 1) * BPH, :],
                                            PT[h][:, :].rearrange("p (m n) -> p m n", m=BPH),
                                            pT_hi[:, parity, h * BPH:(h + 1) * BPH, :].bitcast(F32),
                                            ALU.subtract).then_inc(dv_pT, 1)

            def output(u, i, parity, bank):
                nc.vector.reciprocal(row_inv[:, parity:parity + 1], row_sum[:, bass.ds(i, 1)]).then_inc(dv_inv, 1)
                dve.wait_ge(dv_inv, u * NB + i + 1)
                dve.wait_ge(pe_O, u * NB + i + 1)
                dve.wait_ge(po_resid, u * NB + i + 1)
                rows = xnat[:, bass.ds(u % IMAGES, 1), bass.ds(i, 1), :].rearrange("p a b c -> p (a b c)")
                inv = row_inv[:, parity:parity + 1]
                nc.vector.scalar_tensor_tensor(part_out[:, parity, :], bank[:, C:2 * C], inv, rows,
                                               ALU.mult, ALU.add).then_inc(dv_part, 1)
                dve.wait_ge(dv_part, u * NB + i + 1)
                nc.vector.scalar_tensor_tensor(rows, bank[:, 0:C], inv, part_out[:, parity, :],
                                               ALU.mult, ALU.add).then_inc(dv_O, 1)

            def unit(u, last):
                for q in range(TQ):
                    h, k = divmod(q, KC)
                    dve.wait_ge(ac_t, u * TQ + q + 1)
                    cols = slice(h * BANK, (h + 1) * BANK)
                    nc.vector.scalar_tensor_tensor(t_lo[:, k, cols], T_RING[q][:], att[:, U0 + k:U0 + k + 1],
                                                   t_hi[:, k, cols].bitcast(F32), ALU.add, ALU.subtract
                                                   ).then_inc(dv_t, 1)
                row_max(u, 0, 0)
                for m in range(NB):
                    if not last and m == NB - 1:
                        dve.wait_ge(dv_bn, (u + 1) * NR + NR)
                    v_low(u, m)
                    if m == 0:
                        bias_of(u, 0, 0, first=True)
                    if not last and m % 2 == 0:
                        statistics_of(u + 1, m // 2)
                if not last:
                    channel_statistics(u + 1)
                    group_deviation(u + 1)
                row_max(u, 1, 1)
                bias_of(u, 1, 1, first=True)
                if not last:
                    variance(u + 1)
                p_low(u, 0, 0)
                if not last:
                    affine_map(u + 1)
                    normalise(u + 1)
                with dve.Fori(0, NB // 2 - 1) as j:
                    for k in range(2):
                        i = 2 * j + k
                        row_max(u, i + 2, k)
                        bias_of(u, i + 2, k)
                        p_low(u, i + 1, 1 - k)
                        output(u, i, k, O)
                p_low(u, NB - 1, 1)
                if not last:
                    xn_low(u + 1, 0)
                output(u, NB - 2, 0, X)
                if not last:
                    xn_low(u + 1, 1)
                output(u, NB - 1, 1, O)

            with dve.Fori(0, UNITS - 1) as u:
                unit(u, False)
            unit(UNITS - 1, True)

        @block.tensor
        def _(pe):
            def passes(bank, pairs):
                todo = [(lo_s, hi_m) for (_, lo_s), (hi_m, _) in pairs]
                todo += [p for (hi_s, _), (hi_m, lo_m) in pairs for p in ((hi_s, lo_m), (hi_s, hi_m))]
                for n, (stationary, moving) in enumerate(todo):
                    last = nc.tensor.matmul(bank, stationary, moving, start=(n == 0), stop=(n == len(todo) - 1))
                return last

            def transpose_weight(l, n):
                name, bank = (("wq", T0), ("wk", T1), ("wv", O))[n]
                pe.wait_ge(ld_w[l, name], 16)
                if l:
                    pe.wait_ge(ac_wT, n + 1)
                for kd in range(KC):
                    for kc in range(KC):
                        last = nc.tensor.transpose(bank[:, kd * C + kc * P:kd * C + (kc + 1) * P],
                                                   w_raw[l, name][:, kc, kd * P:(kd + 1) * P], ident[:])
                last.then_inc(pe_wT, 1)

            def A_product(l, mc):
                pe.wait_ge(ac_wT, 3 * l + 2)
                pe.wait_ge(po_bk, l + 1)
                if l:
                    pe.wait_ge(dv_A, mc + 1)
                for kd in range(KC):
                    last = nc.tensor.matmul(S[0][:, mc * BANK:mc * BANK + C + 1], wqT[:, l, kd, mc * P:(mc + 1) * P],
                                            wkT_bk[:, l, kd, :], start=(kd == 0), stop=(kd == KC - 1))
                last.then_inc(pe_A, 1)

            def Wx_product(l, mc):
                pe.wait_ge(ac_wT, 3 * l + 3)
                pe.wait_ge(ld_w[l, "wp"], 16)
                if l:
                    pe.wait_ge(dv_Wx, mc + 1)
                else:
                    pe.wait_ge(ac_xT, NR - KC + mc + 1)
                for kd in range(KC):
                    last = nc.tensor.matmul(S[1][:, mc * BANK:mc * BANK + C], wvT[:, l, kd, mc * P:(mc + 1) * P],
                                            w_raw[l, "wp"][:, kd, :], start=(kd == 0), stop=(kd == KC - 1))
                last.then_inc(pe_Wx, 1)

            def output_bias(l, bank):
                pe.wait_ge(ld_w[l, "wp"], 16)
                r = l * NV + VECTORS.index("bv")
                for kd in range(KC):
                    last = nc.tensor.matmul(bank[:, 0:C], vec_cols[:, kd, r:r + 1].to_broadcast([P, P]),
                                            w_raw[l, "wp"][:, kd, :], start=(kd == 0), stop=(kd == KC - 1))
                last.then_inc(pe_ob, 1)

            def transpose_rows(bank, rows, r):
                for k in range(KC):
                    for i in range(2):
                        last = nc.tensor.transpose(bank[:, (2 * k + i) * P:(2 * k + i + 1) * P],
                                                   rows[:, 2 * r + i, k * P:(k + 1) * P], ident[:])
                last.then_inc(pe_xT, 1)

            def mean_of_groups(v):
                pe.wait_ge(ac_xT, v * NR + NR)
                pe.wait_ge(dv_stat, v * STAT + AGGR)
                nc.tensor.matmul(X[:, 0:KC], group_mean[:], mv[:, :, 0], start=True, stop=True).then_inc(pe_gm, 1)

            def variance_of_groups(v):
                pe.wait_ge(dv_stat, v * STAT + VARC)
                nc.tensor.matmul(X[:, 0:KC], group_mean[:], var_c[:], start=True, stop=True).then_inc(pe_gv, 1)

            pe.wait_ge(po_const, 5)
            transpose_weight(0, 0)
            pe.wait_ge(ld_vec, 16)
            for k in range(KC):
                last = nc.tensor.transpose(O[:, k * LAYERS * NV:(k + 1) * LAYERS * NV],
                                           vec_rows[:, k * P:(k + 1) * P], ident[0:LAYERS * NV, 0:LAYERS * NV])
            last.then_inc(pe_vec, 1)
            transpose_weight(0, 1)
            for r in range(NR):
                pe.wait_ge(ld_x[0][r], 16)
                if r >= 2:
                    pe.wait_ge(ac_xT, r - 1)
                transpose_rows(S[1][:, (r % 2) * BANK:(r % 2 + 1) * BANK], xnat[:, 0], r)
                if r == 2:
                    A_product(0, 0)
            A_product(0, 1)
            pe.wait_ge(dv_vec, 1)
            transpose_weight(0, 2)
            transpose_weight(1, 0)
            transpose_weight(1, 1)
            mean_of_groups(0)
            Wx_product(0, 0)
            variance_of_groups(0)
            Wx_product(0, 1)
            transpose_weight(1, 2)
            pe.wait_ge(dv_stat, VARE)
            output_bias(0, X)
            pe.wait_ge(ac_wT, 6)
            output_bias(1, O)
            for mc in range(KC):
                A_product(1, mc)
            for mc in range(KC):
                Wx_product(1, mc)

            def t_product(u):
                pe.wait_ge(po_unit, u * 2 + 2)
                for q in range(TQ):
                    h, k = divmod(q, KC)
                    cols = slice(h * BANK, (h + 1) * BANK)
                    if k == 0:
                        pe.wait_ge(dv_xl, u * TQ + (h + 1) * KC)
                    if q == 2:
                        pe.wait_ge(dv_O, FIRST + u * NB)
                    passes(T_RING[q][:], [((Ac_hi[:, kc, k * P:(k + 1) * P], Ac_lo[:, kc, k * P:(k + 1) * P]),
                                           (xn_hi[:, kc, cols], xn_lo[:, kc, cols])) for kc in range(KC)]
                           ).then_inc(pe_t, 1)

            def scores(u, i, parity, first=False):
                if first:
                    pe.wait_ge(dv_t, u * TQ + KC)
                    t_block = [t[:, :, i * P:(i + 1) * P] for t in (t_hi, t_lo)]
                else:
                    pe.wait_ge(po_block, (u * (NB - 1) + i - 2) * 2 + 2)
                    pe.wait_ge(ac_P, u * NB + i - 1)
                    t_block = [tb[:, parity] for tb in (tb_hi, tb_lo)]
                todo = []
                for kc in range(KC):
                    todo.append((t_block[1][:, kc, :], xn_hi, kc))
                    todo.append((t_block[0][:, kc, :], xn_lo, kc))
                    todo.append((t_block[0][:, kc, :], xn_hi, kc))
                for n, (stationary, moving, kc) in enumerate(todo):
                    for h in range(HALVES):
                        last = nc.tensor.matmul(S[parity][:, h * BANK:(h + 1) * BANK], stationary,
                                                moving[:, kc, h * BANK:(h + 1) * BANK],
                                                start=(n == 0), stop=(n == len(todo) - 1))
                last.then_inc(pe_S, 1)

            def values(u, m):
                if m < 3:
                    pe.wait_ge(dv_t, u * TQ + m + 1)
                else:
                    pe.wait_ge(dv_V, u * NB + m - 2)
                rows = slice(m * P, (m + 1) * P)
                l = bass.ds(u // IMAGES, 1)
                passes(V_RING[m % 3][:, 0:WX], [((xn_hi[:, kc, rows], xn_lo[:, kc, rows]),
                                                 (Wx_hi[:, l, kc, :].rearrange("p a c -> p (a c)"),
                                                  Wx_lo[:, l, kc, :].rearrange("p a c -> p (a c)")))
                                                for kc in range(KC)]).then_inc(pe_V, 1)

            def next_rows(u, r):
                pe.wait_ge(ac_xstat, u * NR + r + 1)
                if r == 0:
                    pe.wait_ge(dv_t, u * TQ + TQ)
                else:
                    pe.wait_ge(ac_xT, (u + 1) * NR + r)
                transpose_rows(X, xstat, r)

            def transpose_probs(u, i, parity, first=False):
                pe.wait_ge(ac_P, u * NB + i + 1)
                if first:
                    pe.wait_ge(dv_V, u * NB + NB)
                else:
                    pe.wait_ge(dv_pT, (u * NB + i) * HALVES)
                for h in range(HALVES):
                    for m in range(BPH):
                        at = (h * BPH + m) * P
                        last = nc.tensor.transpose(PT[h][:, m * P:(m + 1) * P], probs[:, parity, at:at + P], ident[:])
                    last.then_inc(pe_pT, 1)

            def attend(u, i, parity, bank):
                pe.wait_ge(dv_pT, (u * NB + i) * HALVES + HALVES)
                for m in range(NB):
                    nc.tensor.matmul(bank[:], pT_hi[:, parity, m, :], V[:, m, :], start=(m == 0), stop=False)
                    last = nc.tensor.matmul(bank[:, C:2 * C], pT_lo[:, parity, m, :], V[:, m, 0:C],
                                            start=False, stop=(m == NB - 1))
                last.then_inc(pe_O, 1)

            def unit(u, last):
                t_product(u)
                scores(u, 0, 0, first=True)
                for m in range(NB):
                    values(u, m)
                    if not last and m % 2 == 0:
                        next_rows(u, m // 2)
                scores(u, 1, 1, first=True)
                if not last:
                    mean_of_groups(u + 1)
                transpose_probs(u, 0, 0, first=True)
                if not last:
                    variance_of_groups(u + 1)
                with pe.Fori(0, NB // 2 - 1) as j:
                    for k in range(2):
                        i = 2 * j + k
                        scores(u, i + 2, k)
                        transpose_probs(u, i + 1, 1 - k)
                        pe.wait_ge(dv_O, FIRST + u * NB + i)
                        attend(u, i, k, O)
                transpose_probs(u, NB - 1, 1)
                if not last:
                    pe.wait_ge(dv_stat, (u + 1) * STAT + VARE)
                attend(u, NB - 2, 0, X)
                pe.wait_ge(dv_O, FIRST + u * NB + NB - 2)
                attend(u, NB - 1, 1, O)

            with pe.Fori(0, UNITS - 1) as u:
                unit(u, False)
            unit(UNITS - 1, True)


_L0 = {"gamma": "L0_conv_gamma", "beta": "L0_conv_beta", "wq": "L0_conv_wq", "bq": "L0_conv_bq", "wk": "L0_conv_wk",
       "bk": "L0_conv_bk", "wv": "L0_conv_wv", "bv": "L0_conv_bv", "wp": "L0_conv_wp", "bp": "L0_conv_bp"}
_L1 = {"gamma": "L1_conv_gn_gamma", "beta": "L1_conv_gn_beta", "wq": "L1_conv_wq", "bq": "L1_conv_bq",
       "wk": "L1_conv_wk", "bk": "L1_conv_bk", "wv": "L1_conv_wv", "bv": "L1_conv_bv", "wp": "L1_conv_wo",
       "bp": "L1_conv_bo"}


def kernel(**inputs):
    import numpy as _np
    import concourse.bacc as _bacc
    from concourse import mybir as _mybir
    from concourse.bass_utils import run_bass_kernel_spmd as _run

    nc = _bacc.Bacc("TRN2", target_bir_lowering=False, num_devices=1)
    arrays = {}

    def dram(name, a):
        a = _np.ascontiguousarray(a)
        arrays[f"in_{name}"] = a
        return nc.dram_tensor(f"in_{name}", a.shape, _mybir.dt.from_np(a.dtype), kind="ExternalInput").ap()

    x = dram("x", inputs["x"])
    layers = [{k: dram(names[k], inputs[names[k]]) for k in ("wq", "wk", "wv", "wp")} for names in (_L0, _L1)]
    vectors = dram("vectors", _np.stack([inputs[names[k]] for names in (_L0, _L1) for k in VECTORS]))
    out = nc.dram_tensor("out_0", inputs["x"].shape, _mybir.dt.float32, kind="ExternalOutput").ap()
    two_attention_layers(nc, x.rearrange("b h w c -> b (h w) c"), layers, vectors,
                         out.rearrange("b h w c -> b (h w) c"))
    r = _run(nc, [arrays], core_ids=[0])
    return r.results[0]["out_0"]
```
